# Optimizing a Trainium2 kernel written in Bass

```python
import numpy as np
import jax
import jax.numpy as jnp

def _softmax(x, axis=-1):
    return jax.nn.softmax(x, axis=axis)

def _gelu(x):
    return jax.nn.gelu(x, approximate=True)

def _silu(x):
    return jax.nn.silu(x)

def _sigmoid(x):
    return jax.nn.sigmoid(x)

def _layernorm(x, axis=-1, eps=1e-05):
    m = jnp.mean(x, axis=axis, keepdims=True)
    v = jnp.var(x, axis=axis, keepdims=True)
    return (x - m) / jnp.sqrt(v + eps)

def _scatter_add(tgt, idx, src, axis=0):
    return tgt.at[idx].add(src)

def _segment_sum(src, seg, n):
    return jax.ops.segment_sum(src, seg, n)
kernel_name = 'mk_conv_seq_d2_conv_nchw96_r4_490bd8'

def setup_inputs(seed: int=0):
    np.random.seed(seed)
    _w = jnp.asarray

    def _rec_inputs():
        import jax
        import jax.numpy as jnp
        _gk = jax.random.key(seed)
        x = -0.0002221 + 1 * jax.random.normal(jax.random.fold_in(_gk, 1), (4, 24, 64, 64), jnp.float32)
        return x
    x = _rec_inputs()

    def _L0_conv_setup():
        import jax, jax.numpy as jnp
        from jax import lax
        import numpy as np
        WS = 8
        SHIFT = 4
        NH = 3
        EPS = 1e-05

        def _rel_pos_index(ws):
            coords = np.stack(np.meshgrid(np.arange(ws), np.arange(ws), indexing='ij'))
            cf = coords.reshape(2, -1)
            rel = (cf[:, :, None] - cf[:, None, :]).transpose(1, 2, 0)
            rel[:, :, 0] += ws - 1
            rel[:, :, 1] += ws - 1
            rel[:, :, 0] *= 2 * ws - 1
            return rel.sum(-1)

        def _attn_mask(H, W, ws, shift):
            img = np.zeros((H, W), dtype=np.float32)
            sl = (slice(0, -ws), slice(-ws, -shift), slice(-shift, None))
            cnt = 0
            for h in sl:
                for w in sl:
                    img[h, w] = cnt
                    cnt += 1
            mw = img.reshape(H // ws, ws, W // ws, ws).transpose(0, 2, 1, 3).reshape(-1, ws * ws)
            am = mw[:, None, :] - mw[:, :, None]
            return np.where(am != 0, -100.0, 0.0).astype(np.float32)

        def _layernorm(x, g, b):
            mu = jnp.mean(x, axis=-1, keepdims=True)
            var = jnp.mean(jnp.square(x - mu), axis=-1, keepdims=True)
            return (x - mu) * lax.rsqrt(var + EPS) * g + b

        def _window_partition(x, ws):
            B, H, W, C = x.shape
            x = x.reshape(B, H // ws, ws, W // ws, ws, C).transpose(0, 1, 3, 2, 4, 5)
            return x.reshape(-1, ws * ws, C)

        def _window_reverse(w, ws, B, H, W):
            C = w.shape[-1]
            x = w.reshape(B, H // ws, W // ws, ws, ws, C).transpose(0, 1, 3, 2, 4, 5)
            return x.reshape(B, H, W, C)

        def _forward(x, rpb_table, qkv_w, qkv_b, proj_w, proj_b, norm1_g, norm1_b, norm2_g, norm2_b, pin_w, dw_w, pout_w):
            B, C, H, W = x.shape
            N = WS * WS
            hd = C // NH
            scale = hd ** (-0.5)
            shortcut = x
            xn = _layernorm(x.transpose(0, 2, 3, 1), norm1_g, norm1_b)
            xs = jnp.roll(xn, (-SHIFT, -SHIFT), axis=(1, 2))
            xw = _window_partition(xs, WS)
            Bw = xw.shape[0]
            qkv = (xw @ qkv_w.T + qkv_b).reshape(Bw, N, 3, NH, hd).transpose(2, 0, 3, 1, 4)
            q, k, v = (qkv[0], qkv[1], qkv[2])
            attn = jnp.einsum('bhnd,bhmd->bhnm', q * scale, k)
            rpi = _rel_pos_index(WS).reshape(-1)
            bias = rpb_table[rpi].reshape(N, N, NH).transpose(2, 0, 1)
            attn = attn + bias[None]
            mask = jnp.asarray(_attn_mask(H, W, WS, SHIFT))
            nW = mask.shape[0]
            attn = attn.reshape(B, nW, NH, N, N) + mask[None, :, None]
            attn = jax.nn.softmax(attn.reshape(Bw, NH, N, N), axis=-1)
            out = jnp.einsum('bhnm,bhmd->bhnd', attn, v).transpose(0, 2, 1, 3).reshape(Bw, N, C)
            out = out @ proj_w.T + proj_b
            out = _window_reverse(out, WS, B, H, W)
            out = jnp.roll(out, (SHIFT, SHIFT), axis=(1, 2)).transpose(0, 3, 1, 2)
            x = shortcut + out
            y = _layernorm(x.transpose(0, 2, 3, 1).reshape(B, H * W, C), norm2_g, norm2_b)
            y = y.reshape(B, C, H, W)
            y = jnp.einsum('oc,bchw->bohw', pin_w, y)
            y = lax.conv_general_dilated(y, dw_w, (1, 1), ((1, 1), (1, 1)), dimension_numbers=('NCHW', 'OIHW', 'NCHW'), feature_group_count=y.shape[1])
            h = y.shape[1] // 2
            y = jax.nn.gelu(y[:, :h], approximate=False) * y[:, h:]
            y = jnp.einsum('oc,bchw->bohw', pout_w, y)
            return x + y
        key = jax.random.key(seed)
        ks = jax.random.split(key, 8)
        dim, hid = (24, int(24 * 2.66))
        return {'x': jax.random.normal(ks[0], (4, dim, 64, 64), jnp.float32), 'rpb_table': jax.random.normal(ks[1], (225, NH), jnp.float32) * 0.02, 'qkv_w': jax.random.normal(ks[2], (3 * dim, dim), jnp.float32) * 0.02, 'qkv_b': jnp.zeros((3 * dim,), jnp.float32), 'proj_w': jax.random.normal(ks[3], (dim, dim), jnp.float32) * 0.02, 'proj_b': jnp.zeros((dim,), jnp.float32), 'norm1_g': jnp.ones((dim,), jnp.float32), 'norm1_b': jnp.zeros((dim,), jnp.float32), 'norm2_g': jnp.ones((dim,), jnp.float32), 'norm2_b': jnp.zeros((dim,), jnp.float32), 'pin_w': jax.random.normal(ks[4], (2 * hid, dim), jnp.float32) * 0.02, 'dw_w': jax.random.normal(ks[5], (2 * hid, 1, 3, 3), jnp.float32) * 0.02, 'pout_w': jax.random.normal(ks[6], (dim, hid), jnp.float32) * 0.02}
    _L0_conv_all = _L0_conv_setup()
    _L0_conv_in = {k: v for k, v in _L0_conv_all.items() if k in ('rpb_table', 'qkv_w', 'qkv_b', 'proj_w', 'proj_b', 'norm1_g', 'norm1_b', 'norm2_g', 'norm2_b', 'pin_w', 'dw_w', 'pout_w')}
    del _L0_conv_all

    def _L1_conv_setup():
        import jax, jax.numpy as jnp
        import numpy as np
        from jax import lax
        EPS = 1e-05
        K = 2

        def conv1x1(x, w, b):
            return jnp.einsum('bchw,oc->bohw', x, w) + b[None, :, None, None]

        def bn(x, g, b, m, v):
            scale = g * lax.rsqrt(v + EPS)
            return (x - m[None, :, None, None]) * scale[None, :, None, None] + b[None, :, None, None]

        def mrconv_xj(x, k):
            H, W = (x.shape[2], x.shape[3])

            def make_step(axis):

                def step(xj, s):
                    return (jnp.maximum(xj, x - jnp.roll(x, s, axis=axis)), None)
                return step
            shifts_h = jnp.arange(1, (H - 1) // k + 1) * k
            shifts_w = jnp.arange(1, (W - 1) // k + 1) * k
            xj, _ = lax.scan(make_step(2), jnp.zeros_like(x), shifts_h)
            xj, _ = lax.scan(make_step(3), xj, shifts_w)
            return xj
        key = jax.random.key(seed)
        ks = jax.random.split(key, 24)
        dim = 24
        B, H, W = (16, 28, 28)
        d2, d4 = (2 * dim, 4 * dim)

        def r(k, sh, s=0.05):
            return jax.random.normal(k, sh, jnp.float32) * s
        return dict(x=jax.random.normal(ks[0], (B, dim, H, W), jnp.float32), w1=r(ks[1], (dim, dim)), b1=r(ks[2], (dim,)), g1=1.0 + r(ks[3], (dim,)), be1=r(ks[4], (dim,)), m1=r(ks[5], (dim,)), v1=1.0 + 0.1 * jax.random.uniform(ks[6], (dim,)), wg=r(ks[7], (d2, d2)), bg=r(ks[8], (d2,)), gg=1.0 + r(ks[9], (d2,)), beg=r(ks[10], (d2,)), mg=r(ks[11], (d2,)), vg=1.0 + 0.1 * jax.random.uniform(ks[12], (d2,)), w2=r(ks[13], (dim, d2)), b2=r(ks[14], (dim,)), g2=1.0 + r(ks[15], (dim,)), be2=r(ks[16], (dim,)), m2=r(ks[17], (dim,)), v2=1.0 + 0.1 * jax.random.uniform(ks[18], (dim,)), wf1=r(ks[19], (d4, dim)), bf1=r(ks[20], (d4,)), wf2=r(ks[21], (dim, d4)), bf2=r(ks[22], (dim,)))
    _L1_conv_all = _L1_conv_setup()
    _L1_conv_in = {k: v for k, v in _L1_conv_all.items() if k in ('w1', 'b1', 'g1', 'be1', 'm1', 'v1', 'wg', 'bg', 'gg', 'beg', 'mg', 'vg', 'w2', 'b2', 'g2', 'be2', 'm2', 'v2', 'wf1', 'bf1', 'wf2', 'bf2')}
    del _L1_conv_all
    return {'x': x, 'L0_conv_rpb_table': _L0_conv_in['rpb_table'], 'L0_conv_qkv_w': _L0_conv_in['qkv_w'], 'L0_conv_qkv_b': _L0_conv_in['qkv_b'], 'L0_conv_proj_w': _L0_conv_in['proj_w'], 'L0_conv_proj_b': _L0_conv_in['proj_b'], 'L0_conv_norm1_g': _L0_conv_in['norm1_g'], 'L0_conv_norm1_b': _L0_conv_in['norm1_b'], 'L0_conv_norm2_g': _L0_conv_in['norm2_g'], 'L0_conv_norm2_b': _L0_conv_in['norm2_b'], 'L0_conv_pin_w': _L0_conv_in['pin_w'], 'L0_conv_dw_w': _L0_conv_in['dw_w'], 'L0_conv_pout_w': _L0_conv_in['pout_w'], 'L1_conv_w1': _L1_conv_in['w1'], 'L1_conv_b1': _L1_conv_in['b1'], 'L1_conv_g1': _L1_conv_in['g1'], 'L1_conv_be1': _L1_conv_in['be1'], 'L1_conv_m1': _L1_conv_in['m1'], 'L1_conv_v1': _L1_conv_in['v1'], 'L1_conv_wg': _L1_conv_in['wg'], 'L1_conv_bg': _L1_conv_in['bg'], 'L1_conv_gg': _L1_conv_in['gg'], 'L1_conv_beg': _L1_conv_in['beg'], 'L1_conv_mg': _L1_conv_in['mg'], 'L1_conv_vg': _L1_conv_in['vg'], 'L1_conv_w2': _L1_conv_in['w2'], 'L1_conv_b2': _L1_conv_in['b2'], 'L1_conv_g2': _L1_conv_in['g2'], 'L1_conv_be2': _L1_conv_in['be2'], 'L1_conv_m2': _L1_conv_in['m2'], 'L1_conv_v2': _L1_conv_in['v2'], 'L1_conv_wf1': _L1_conv_in['wf1'], 'L1_conv_bf1': _L1_conv_in['bf1'], 'L1_conv_wf2': _L1_conv_in['wf2'], 'L1_conv_bf2': _L1_conv_in['bf2']}

def reference(x, L0_conv_rpb_table, L0_conv_qkv_w, L0_conv_qkv_b, L0_conv_proj_w, L0_conv_proj_b, L0_conv_norm1_g, L0_conv_norm1_b, L0_conv_norm2_g, L0_conv_norm2_b, L0_conv_pin_w, L0_conv_dw_w, L0_conv_pout_w, L1_conv_w1, L1_conv_b1, L1_conv_g1, L1_conv_be1, L1_conv_m1, L1_conv_v1, L1_conv_wg, L1_conv_bg, L1_conv_gg, L1_conv_beg, L1_conv_mg, L1_conv_vg, L1_conv_w2, L1_conv_b2, L1_conv_g2, L1_conv_be2, L1_conv_m2, L1_conv_v2, L1_conv_wf1, L1_conv_bf1, L1_conv_wf2, L1_conv_bf2):
    import jax
    import jax.numpy as jnp

    def _L0_conv_ref(x, rpb_table, qkv_w, qkv_b, proj_w, proj_b, norm1_g, norm1_b, norm2_g, norm2_b, pin_w, dw_w, pout_w):
        import jax, jax.numpy as jnp
        from jax import lax
        import numpy as np
        WS = 8
        SHIFT = 4
        NH = 3
        EPS = 1e-05

        def _rel_pos_index(ws):
            coords = np.stack(np.meshgrid(np.arange(ws), np.arange(ws), indexing='ij'))
            cf = coords.reshape(2, -1)
            rel = (cf[:, :, None] - cf[:, None, :]).transpose(1, 2, 0)
            rel[:, :, 0] += ws - 1
            rel[:, :, 1] += ws - 1
            rel[:, :, 0] *= 2 * ws - 1
            return rel.sum(-1)

        def _attn_mask(H, W, ws, shift):
            img = np.zeros((H, W), dtype=np.float32)
            sl = (slice(0, -ws), slice(-ws, -shift), slice(-shift, None))
            cnt = 0
            for h in sl:
                for w in sl:
                    img[h, w] = cnt
                    cnt += 1
            mw = img.reshape(H // ws, ws, W // ws, ws).transpose(0, 2, 1, 3).reshape(-1, ws * ws)
            am = mw[:, None, :] - mw[:, :, None]
            return np.where(am != 0, -100.0, 0.0).astype(np.float32)

        def _layernorm(x, g, b):
            mu = jnp.mean(x, axis=-1, keepdims=True)
            var = jnp.mean(jnp.square(x - mu), axis=-1, keepdims=True)
            return (x - mu) * lax.rsqrt(var + EPS) * g + b

        def _window_partition(x, ws):
            B, H, W, C = x.shape
            x = x.reshape(B, H // ws, ws, W // ws, ws, C).transpose(0, 1, 3, 2, 4, 5)
            return x.reshape(-1, ws * ws, C)

        def _window_reverse(w, ws, B, H, W):
            C = w.shape[-1]
            x = w.reshape(B, H // ws, W // ws, ws, ws, C).transpose(0, 1, 3, 2, 4, 5)
            return x.reshape(B, H, W, C)

        def _forward(x, rpb_table, qkv_w, qkv_b, proj_w, proj_b, norm1_g, norm1_b, norm2_g, norm2_b, pin_w, dw_w, pout_w):
            B, C, H, W = x.shape
            N = WS * WS
            hd = C // NH
            scale = hd ** (-0.5)
            shortcut = x
            xn = _layernorm(x.transpose(0, 2, 3, 1), norm1_g, norm1_b)
            xs = jnp.roll(xn, (-SHIFT, -SHIFT), axis=(1, 2))
            xw = _window_partition(xs, WS)
            Bw = xw.shape[0]
            qkv = (xw @ qkv_w.T + qkv_b).reshape(Bw, N, 3, NH, hd).transpose(2, 0, 3, 1, 4)
            q, k, v = (qkv[0], qkv[1], qkv[2])
            attn = jnp.einsum('bhnd,bhmd->bhnm', q * scale, k)
            rpi = _rel_pos_index(WS).reshape(-1)
            bias = rpb_table[rpi].reshape(N, N, NH).transpose(2, 0, 1)
            attn = attn + bias[None]
            mask = jnp.asarray(_attn_mask(H, W, WS, SHIFT))
            nW = mask.shape[0]
            attn = attn.reshape(B, nW, NH, N, N) + mask[None, :, None]
            attn = jax.nn.softmax(attn.reshape(Bw, NH, N, N), axis=-1)
            out = jnp.einsum('bhnm,bhmd->bhnd', attn, v).transpose(0, 2, 1, 3).reshape(Bw, N, C)
            out = out @ proj_w.T + proj_b
            out = _window_reverse(out, WS, B, H, W)
            out = jnp.roll(out, (SHIFT, SHIFT), axis=(1, 2)).transpose(0, 3, 1, 2)
            x = shortcut + out
            y = _layernorm(x.transpose(0, 2, 3, 1).reshape(B, H * W, C), norm2_g, norm2_b)
            y = y.reshape(B, C, H, W)
            y = jnp.einsum('oc,bchw->bohw', pin_w, y)
            y = lax.conv_general_dilated(y, dw_w, (1, 1), ((1, 1), (1, 1)), dimension_numbers=('NCHW', 'OIHW', 'NCHW'), feature_group_count=y.shape[1])
            h = y.shape[1] // 2
            y = jax.nn.gelu(y[:, :h], approximate=False) * y[:, h:]
            y = jnp.einsum('oc,bchw->bohw', pout_w, y)
            return x + y
        return _forward(x, rpb_table, qkv_w, qkv_b, proj_w, proj_b, norm1_g, norm1_b, norm2_g, norm2_b, pin_w, dw_w, pout_w)

    def _L1_conv_ref(x, w1, b1, g1, be1, m1, v1, wg, bg, gg, beg, mg, vg, w2, b2, g2, be2, m2, v2, wf1, bf1, wf2, bf2):
        import jax, jax.numpy as jnp
        import numpy as np
        from jax import lax
        EPS = 1e-05
        K = 2

        def conv1x1(x, w, b):
            return jnp.einsum('bchw,oc->bohw', x, w) + b[None, :, None, None]

        def bn(x, g, b, m, v):
            scale = g * lax.rsqrt(v + EPS)
            return (x - m[None, :, None, None]) * scale[None, :, None, None] + b[None, :, None, None]

        def mrconv_xj(x, k):
            H, W = (x.shape[2], x.shape[3])

            def make_step(axis):

                def step(xj, s):
                    return (jnp.maximum(xj, x - jnp.roll(x, s, axis=axis)), None)
                return step
            shifts_h = jnp.arange(1, (H - 1) // k + 1) * k
            shifts_w = jnp.arange(1, (W - 1) // k + 1) * k
            xj, _ = lax.scan(make_step(2), jnp.zeros_like(x), shifts_h)
            xj, _ = lax.scan(make_step(3), xj, shifts_w)
            return xj
        shortcut = x
        h = bn(conv1x1(x, w1, b1), g1, be1, m1, v1)
        xj = mrconv_xj(h, K)
        h = jnp.concatenate([h, xj], axis=1)
        h = jax.nn.gelu(bn(conv1x1(h, wg, bg), gg, beg, mg, vg), approximate=False)
        h = bn(conv1x1(h, w2, b2), g2, be2, m2, v2) + shortcut
        h = conv1x1(jax.nn.gelu(conv1x1(h, wf1, bf1), approximate=False), wf2, bf2)
        return h

    def _gn(v, G=32, eps=1e-05):
        B_, C_, H_, W_ = v.shape
        g = v.reshape(B_, G, C_ // G, H_, W_)
        m = jnp.mean(g, axis=(2, 3, 4), keepdims=True)
        s = jnp.var(g, axis=(2, 3, 4), keepdims=True)
        return ((g - m) / jnp.sqrt(s + eps)).reshape(v.shape)

    def _ln_c(v, eps=1e-06):
        m = jnp.mean(v, axis=1, keepdims=True)
        s = jnp.var(v, axis=1, keepdims=True)
        return (v - m) / jnp.sqrt(s + eps)

    def _ln_t(v, eps=1e-05):
        m = jnp.mean(v, axis=-1, keepdims=True)
        s = jnp.var(v, axis=-1, keepdims=True)
        return (v - m) / jnp.sqrt(s + eps)

    def _to_tokens(v):
        B_, C_, H_, W_ = v.shape
        return v.reshape(B_, C_, H_ * W_).transpose(0, 2, 1)

    def _from_tokens(t, like):
        B_, C_, H_, W_ = like.shape
        return t.transpose(0, 2, 1).reshape(B_, C_, H_, W_)
    x = _L0_conv_ref(x, L0_conv_rpb_table, L0_conv_qkv_w, L0_conv_qkv_b, L0_conv_proj_w, L0_conv_proj_b, L0_conv_norm1_g, L0_conv_norm1_b, L0_conv_norm2_g, L0_conv_norm2_b, L0_conv_pin_w, L0_conv_dw_w, L0_conv_pout_w)
    x = _L1_conv_ref(x, L1_conv_w1, L1_conv_b1, L1_conv_g1, L1_conv_be1, L1_conv_m1, L1_conv_v1, L1_conv_wg, L1_conv_bg, L1_conv_gg, L1_conv_beg, L1_conv_mg, L1_conv_vg, L1_conv_w2, L1_conv_b2, L1_conv_g2, L1_conv_be2, L1_conv_m2, L1_conv_v2, L1_conv_wf1, L1_conv_bf1, L1_conv_wf2, L1_conv_bf2)
    return x

_drawn_inputs = setup_inputs


def setup_inputs(seed=0):
    import zlib

    import numpy as np

    out = dict(_drawn_inputs(seed))
    spreads = {'L0_conv_qkv_b': (0.0, 0.8),
     'L0_conv_proj_b': (0.0, 0.1),
     'L0_conv_norm1_g': (1.0, 0.6),
     'L0_conv_norm1_b': (0.0, 0.8),
     'L0_conv_norm2_g': (1.0, 0.6),
     'L0_conv_norm2_b': (0.0, 0.8)}
    factors = {'L0_conv_rpb_table': 31.293,
     'L0_conv_qkv_w': 8.0,
     'L0_conv_proj_w': 6.584,
     'L0_conv_pin_w': 8.0,
     'L0_conv_dw_w': 8.0,
     'L0_conv_pout_w': 8.0,
     'L1_conv_w1': 4.112,
     'L1_conv_b1': 8.0,
     'L1_conv_g1': 33.818,
     'L1_conv_be1': 34.225,
     'L1_conv_m1': 8.0,
     'L1_conv_v1': 200.0,
     'L1_conv_bg': 8.0,
     'L1_conv_gg': 29.325,
     'L1_conv_beg': 7.11,
     'L1_conv_mg': 8.0,
     'L1_conv_vg': 200.0,
     'L1_conv_g2': 44.972,
     'L1_conv_v2': 200.0,
     'L1_conv_be2': 6.438}
    for name, (base, spread) in spreads.items():
        noise = np.random.default_rng([zlib.crc32(name.encode()), seed]).standard_normal(out[name].shape)
        drawn = base * np.exp(spread * noise) if base else spread * noise
        out[name] = jnp.asarray(drawn.astype(out[name].dtype))
    for name, factor in factors.items():
        out[name] = (out[name] * factor).astype(out[name].dtype)
    return out
```

```python
from contextlib import ExitStack

import concourse.bass as bass
from concourse import mybir

F32 = mybir.dt.float32
F32R = mybir.dt.float32r
ALU = mybir.AluOpType
ACT = mybir.ActivationFunctionType
AX = mybir.AxisListType

B, C, H, W = 4, 24, 64, 64
NT = H * W
WS, SHIFT = 8, 4
NH, HD = 3, 8
HID = 63
BC = B * C
G2 = 2 * C
F4 = 4 * C
CH = 512
NCH = NT // CH
WT = WS * WS
NREG = 4
KX = BC + 1 + NREG
XP = W + SHIFT
PW = W + 2
PL = (H - 1) * PW + W
TA, TB = 5, 4
MASKED = -100.0
LN_EPS, BN_EPS = 1e-5, 1e-5

PACK = {
    "wq": (KX, 128), "wk": (KX, 128), "wv": (KX, BC), "scales": (128, 4),
    "rpb": (WT, NH * WT), "posi": (128, 128), "eye": (128, 128),
    "center": (BC, BC), "avg": (BC, BC), "wproj": (65, 2 * BC), "vecs": (BC, 17),
    "vecs_g": (BC, 5), "bf1": (128, 3), "pin": (C * TA, 127), "dwa": (C * TA, 127), "dwb": (C * TB, 127),
    "pout": (128, 2 * BC), "w1": (BC, BC), "wgh": (BC, 2 * BC), "wgx": (BC, 2 * BC),
    "w2": (BC, 2 * BC), "wf1": (BC, B * F4), "wf2": (128, 3 * BC),
}
PACK_AT, _at = {}, 0
for _name, (_r, _c) in PACK.items():
    PACK_AT[_name] = _at
    _at += _c
PACK_W = _at
(V_N1G, V_N1B, V_N2G, V_N2B, V_B1, V_G1, V_BE1, V_M1, V_V1, V_B2, V_G2, V_BE2, V_M2, V_V2, V_BF2,
 V_EPS, V_BNEPS) = range(17)


def build(nc, xw, feat, pack, out):
    scratch = nc.dram_tensor("scratch", [B, C * NT], F32, kind="Internal").ap()

    with ExitStack() as ctx:
        def sb(stack, name, shape, dt=F32):
            return stack.enter_context(nc.sbuf_tensor(name, shape, dt))

        def sem(name):
            return ctx.enter_context(nc.semaphore(name))

        psum = ctx.enter_context(nc.psum_tensor("psum", [128, 8 * 512], F32))

        def bank(n, cols=512):
            return psum[:, 512 * n:512 * n + cols]

        pk = sb(ctx, "pk", [128, PACK_W])
        x1 = sb(ctx, "x1", [BC, XP, XP])
        small = sb(ctx, "small", [128, 16])
        wca = sb(ctx, "wca", [C * TA, 127])
        wcb = sb(ctx, "wcb", [C * TB, 127])

        def wt(name, c0=0, c1=None):
            r, c = PACK[name]
            a = PACK_AT[name]
            return pk[0:r, a + c0:a + (c if c1 is None else c1)]

        def vec(n):
            return wt("vecs", n, n + 1)

        x1_live = x1[:, 0:H, 0:W]

        att = ExitStack()
        xin = sb(att, "xin", [BC, NT])
        xn = sb(att, "xn", [KX, NT])
        sq = sb(att, "sq", [BC, 4, CH])
        rs = sb(att, "rs", [BC, 4, CH])
        biasr = sb(att, "biasr", [128, 2, 2, NH * WT], F32R)
        posr = sb(att, "posr", [128, 128], F32R)
        xs = sb(att, "xs", [KX, 2, CH])
        qs = sb(att, "qs", [128, 2, CH])
        stq = sb(att, "stq", [128, 2, 2, WS, 128])
        kmv = sb(att, "kmv", [128, 2, WS, NH, WT])
        stv = sb(att, "stv", [128, 2, 2, WS // 2, B, 2, 128])
        diff = sb(att, "diff", [128, 2, 2, 2 * NH * WT])
        mx = sb(att, "mx", [128, 2, 2 * NH])
        pt = sb(att, "pt", [128, 2, 768])
        rz = sb(att, "rz", [64, 2, CH])
        on = sb(att, "on", [65, 2, CH])
        att.close()

        late = ExitStack()
        yn = sb(late, "yn", [BC, NT])
        yt = sb(late, "yt", [128, B, 32, C])
        pad = sb(late, "pad", [BC, PW, PW])
        sta = sb(late, "sta", [C * TA, 2, PL + 2])
        stb = sb(late, "stb", [C * TB, 2, PL + 2])
        gated = sb(late, "gated", [128, 2, NT])
        sq2 = sb(late, "sq2", [BC, 4, CH])
        rs2 = sb(late, "rs2", [BC, 4, CH])
        gel = sb(late, "gel", [HID, 4, CH])
        late.close()
        last = ExitStack()
        x2 = sb(last, "x2", [BC, NT])
        h = sb(last, "h", [BC, NT])
        hmin = sb(last, "hmin", [BC, 2, W])
        wmin = sb(last, "wmin", [BC, H, 2])
        near = sb(last, "near", [BC, 2, 8, W])
        xj = sb(last, "xj", [BC, 2, CH])
        gg = sb(last, "gg", [BC, 2, 2, CH])
        x3 = sb(last, "x3", [BC, 2, CH])
        gf = sb(last, "gf", [128, 2, 3, CH])
        yo = sb(last, "yo", [BC, 2, CH])
        last.close()

        pack_in, x_in, feat_in = sem("pack_in"), sem("x_in"), sem("feat_in")
        zeroed = sem("zeroed")
        bias_high, bias_ready = sem("bias_high"), sem("bias_ready")
        roots_ready, folding, folded = sem("roots_ready"), sem("folding"), sem("folded")
        shift_made, shift_ready = sem("shift_made"), sem("shift_ready")
        centered, squared, varied, rooted, inverted, scaled, normed = (
            sem(n) for n in ("centered", "squared", "varied", "rooted", "inverted", "scaled", "normed"))
        xs_ready, q_made, k_made, qs_ready, kmv_ready, stq_ready = (
            sem(n) for n in ("xs_ready", "q_made", "k_made", "qs_ready", "kmv_ready", "stq_ready"))
        v0_made, v1_made, stv_ready = sem("v0_made"), sem("v1_made"), sem("stv_ready")
        scores_made, max_ready, diff_ready, turned, probs_ready, mixed = (
            sem(n) for n in ("scores_made", "max_ready", "diff_ready", "turned", "probs_ready", "mixed"))
        rz_ready, on_ready, projected, x1_ready = (
            sem(n) for n in ("rz_ready", "on_ready", "projected", "x1_ready"))
        wrapped_right, wrap_ready = sem("wrapped_right"), sem("wrap_ready")
        centered2, squared2, varied2, rooted2, inverted2, scaled2, normed2 = (
            sem(n) for n in ("centered2", "squared2", "varied2", "rooted2", "inverted2", "scaled2", "normed2"))
        yt_turned, drained, pad_zero = sem("yt_turned"), sem("drained"), sem("pad_zero")
        scratch_in = [sem(f"scratch_in{b}") for b in range(B)]
        pad_in = [sem(f"pad_in{b}") for b in range(B)]
        stack_in = [sem(f"stack_in{j}") for j in range(2)]
        conv_made, gelu_ready = sem("conv_made"), sem("gelu_ready")
        pout_made, x2_ready, w1_made, h_ready = sem("pout_made"), sem("x2_ready"), sem("w1_made"), sem("h_ready")
        hmin_ready = sem("hmin_ready")
        near_ready, xj_ready, wg_made, gg_ready = (
            sem(n) for n in ("near_ready", "xj_ready", "wg_made", "gg_ready"))
        w2_made, x3_ready, wf1_made, gf_ready, wf2_made, yo_ready = (
            sem(n) for n in ("w2_made", "x3_ready", "wf1_made", "gf_ready", "wf2_made", "yo_ready"))
        stored = [sem(f"stored{par}") for par in range(2)]

        S1, T1, S2, T2, SG, TG, BF = 0, 1, 2, 3, 4, 5, 6
        R1, R2, RG = 9, 10, 11

        def col(n, rows=BC):
            return small[0:rows, n:n + 1]

        def wait(eng, s, count):
            if isinstance(count, int) and count <= 0:
                return
            eng.wait_ge(s, count)

        def chunk(buf, n):
            return buf[:, bass.ts(n, CH)]

        def rows8(img, n):
            return img[:, bass.ts(n, 8), 0:W]

        block = ctx.enter_context(nc.Block())

        @block.sync
        def _(sp):
            sp.dma_start(pk[:, :], pack).then_inc(pack_in, 16)
            sp.dma_start(xin[:, :], xw).then_inc(x_in, 16)
            sp.dma_start(xn[BC:KX, :], feat).then_inc(feat_in, 16)
            sp.wait_ge(drained, 8)
            for b in range(B):
                sp.dma_start(scratch[b].rearrange("(p n) -> p n", p=128),
                             yt[:, b, :, :].rearrange("p j c -> p (j c)")).then_inc(scratch_in[b], 16)
            sp.wait_ge(pad_zero, 1)
            for b in range(B):
                sp.wait_ge(scratch_in[b], 16)
                sp.dma_start(pad[C * b:C * b + C, 1:1 + H, 1:1 + W],
                             scratch[b].rearrange("(c h w) -> c h w", c=C, h=H)).then_inc(pad_in[b], 16)
            for b in range(B):
                sp.wait_ge(pad_in[b], 16)
                if b >= 2:
                    sp.wait_ge(conv_made, NCH * (b - 1))
                src = pad[C * b:C * b + C].rearrange("c h w -> c (h w)")
                for t in range(TA + TB):
                    stack, at = (sta, t) if t < TA else (stb, t - TA)
                    off = (t // 3) * PW + t % 3
                    sp.dma_start(stack[C * at:C * at + C, b % 2, 0:PL], src[:, off:off + PL])\
                        .then_inc(stack_in[b % 2], 16)
            out_rows = out.rearrange("b c h w -> (b c) (h w)")
            for c in range(NCH):
                sp.wait_ge(yo_ready, c + 1)
                sp.dma_start(out_rows[:, c * CH:(c + 1) * CH], yo[:, c % 2, :]).then_inc(stored[c % 2], 16)
            for par in range(2):
                sp.wait_ge(stored[par], 16 * NCH // 2)

        @block.gpsimd
        def _(pool):
            g = nc.gpsimd
            g.memset(stq[:], 0.0)
            g.memset(stv[:], 0.0).then_inc(zeroed, 1)
            pool.wait_ge(zeroed, 1)
            g.memset(on[64:65, :, :], 1.0)
            for par in range(2):
                for odd in range(2):
                    for j in range(2):
                        at = 64 + 32 * j
                        blocks = stv[:, par, odd].rearrange("k w (p j) n m -> k j n (w p) m", j=2)
                        for half in range(2):
                            rows = slice(64 * half, 64 * half + 64)
                            cut = at + HD * (half ^ odd)
                            g.memset(blocks[rows, j, 0, :, cut:cut + HD], 1.0)
                        rows = slice(64 * odd, 64 * odd + 64)
                        m = g.memset(blocks[rows, j, 1, :, at + 2 * HD:at + 32], 1.0)
            m.then_inc(zeroed, 1)

            def block_q(m, par):
                pool.wait_ge(kmv_ready, m + 1)
                for b in range(B):
                    c = g.tensor_copy(stq[32 * b:32 * b + 32, par, b // 2, :, 64 * (b % 2):64 * (b % 2) + 64],
                                      qs[32 * b:32 * b + 32, par, :].rearrange("p (w t) -> p w t", t=WT))
                c.then_inc(stq_ready, 1)

            pool.wait_ge(zeroed, 2)
            for m in range(NCH):
                block_q(m, m % 2)
            pool.wait_ge(stq_ready, NCH)
            pool.wait_ge(x1_ready, NCH)
            g.memset(pad[:], 0.0).then_inc(pad_zero, 1)
            pool.wait_ge(pad_zero, 1)
            g.memset(gated[:], 0.0).then_inc(pad_zero, 1)
            def sub_near(c, par):
                pool.wait_ge(near_ready, 2 * (c + 1))
                wait(pool, wg_made, c - 1)
                g.tensor_tensor(xj[:, par, :], chunk(h, c), near[:, par].rearrange("p r w -> p (r w)"),
                                ALU.subtract).then_inc(xj_ready, 1)

            sub_near(0, 0)
            sub_near(1, 1)
            with pool.Fori(1, 4) as i:
                for u in range(2):
                    sub_near(2 * i + u, u)

        @block.tensor
        def _(pe):
            mm = nc.tensor.matmul

            def norm_chunks(i, src, made, sqr, squares, squared_, varied_, scaled_):
                for u in range(4):
                    n = 4 * i + u
                    if not (isinstance(i, int) and i == 0):
                        pe.wait_ge(scaled_, n - 3)
                    mm(bank(u)[0:BC], wt("center"), src(n), start=True, stop=True).then_inc(made, 1)
                for u in range(4):
                    n = 4 * i + u
                    pe.wait_ge(squared_, n + 1)
                    mm(bank(4 + u)[0:BC], wt("avg"), squares[:, u, :], start=True, stop=True)\
                        .then_inc(varied_, 1)

            pe.wait_ge(pack_in, 16)
            pe.wait_ge(x_in, 16)
            for i in range(2):
                norm_chunks(i, lambda n: chunk(xin, n), centered, None, sq, squared, varied, scaled)

            def make_qk(m, par):
                pe.wait_ge(xs_ready, m + 1)
                wait(pe, x1_ready, m - 2)
                mm(bank(6), wt("wq"), xs[:, par, :], start=True, stop=True).then_inc(q_made, 1)
                wait(pe, stv_ready, m)
                mm(bank(7), wt("wk"), xs[:, par, :], start=True, stop=True).then_inc(k_made, 1)

            def make_v(m, par):
                for odd, (free, made) in enumerate(((qs_ready, v0_made), (kmv_ready, v1_made))):
                    pe.wait_ge(free, m + 1)
                    for w in range(WS // 2):
                        t0 = (2 * w + odd) * WT
                        l = mm(bank(6 + odd)[0:WT, BC * w:BC * w + BC], xs[:, par, t0:t0 + WT], wt("wv"),
                               start=True, stop=True)
                    l.then_inc(made, 1)

            def scores(m, w, par):
                n = WS * m + w
                if w == 0:
                    pe.wait_ge(stq_ready, m + 1)
                    pe.wait_ge(kmv_ready, m + 1)
                wait(pe, diff_ready, n - 1)
                s = bank(w % 2, 2 * NH * WT)
                mm(s, posr[:, :], biasr[:, w % 2].rearrange("k p n -> k (p n)"), start=True, stop=True)
                for p in range(2):
                    l = mm(s[:, NH * WT * p:NH * WT * (p + 1)], stq[:, par, p, w, :],
                           kmv[:, par, w, :, :].rearrange("k h n -> k (h n)"), start=False, stop=True,
                           skip_group_check=True)
                l.then_inc(scores_made, 1)

            def turn(t, w0):
                pe.wait_ge(diff_ready, 2 * (t + 1))
                wait(pe, probs_ready, t)
                for p in range(2):
                    for k in range(3):
                        at = 384 * p + 128 * k
                        l = nc.tensor.transpose(psum[:, 1024 + at:1024 + at + 128],
                                                diff[:, (w0 // 2) % 2, p, 128 * k:128 * k + 128], wt("eye"))
                l.then_inc(turned, 1)

            def mix(m, l, par):
                t, w0 = 4 * m + l, 2 * l
                if l == 0:
                    pe.wait_ge(stv_ready, m + 1)
                if l % 2 == 0:
                    wait(pe, on_ready, 2 * m + l // 2 - 1)
                pe.wait_ge(probs_ready, t + 1)
                pp = (w0 // 2) % 2
                o = bank(4 + (w0 // 4) % 2)
                for odd in range(2):
                    for p in range(2):
                        dst = o[:, 256 * p + WT * (w0 % 4 + odd):256 * p + WT * (w0 % 4 + odd + 1)]
                        for j in range(2):
                            v = stv[:, par, odd, w0 // 2, 2 * p + j]
                            at = 384 * p + 256 * odd + WT * j
                            mm(dst, v[:, 0, :], pt[:, pp, at:at + WT], start=(j == 0), stop=False)
                            at = 384 * p + 128 + WT * j
                            l = mm(dst, v[:, 1, :], pt[:, pp, at:at + WT], start=False, stop=(j == 1))
                l.then_inc(mixed, 1)

            def project(m):
                pe.wait_ge(on_ready, 2 * m + 2)
                for half in range(2):
                    for p in range(2):
                        l = mm(bank(6)[0:BC, 256 * half:256 * half + 256],
                               wt("wproj", BC * p, BC * p + BC), on[:, half, 256 * p:256 * p + 256],
                               start=(p == 0), stop=(p == 1))
                l.then_inc(projected, 1)

            def attend(m, par, before=True, after=True):
                for l in range(4):
                    t = 4 * m + l
                    if after or l < 3:
                        turn(t + 1, (2 * l + 2) % WS)
                    if after or l < 2:
                        for e in range(2):
                            if l < 2:
                                scores(m, 2 * l + 4 + e, par)
                            else:
                                scores(m + 1, 2 * l - 4 + e, 1 - par)
                    if l == 0 and after:
                        make_qk(m + 1, 1 - par)
                    if l == 1 and after:
                        make_v(m + 1, 1 - par)
                    if l == 2 and before:
                        pe.wait_ge(stv_ready, m + 2 if after else m + 1)
                        project(m - 1)
                    mix(m, l, par)

            make_qk(0, 0)
            make_v(0, 0)
            pe.wait_ge(bias_ready, 1)
            pe.wait_ge(zeroed, 2)
            scores(0, 0, 0)
            scores(0, 1, 0)
            turn(0, 0)
            scores(0, 2, 0)
            scores(0, 3, 0)
            attend(0, 0, before=False)
            with pe.Fori(0, 3) as i:
                attend(2 * i + 1, 1)
                attend(2 * i + 2, 0)
            attend(7, 1, after=False)
            project(7)

            pe.wait_ge(wrap_ready, 1)
            for i in range(2):
                norm_chunks(i, lambda n: rows8(x1, n), centered2, None, sq2, squared2, varied2, scaled2)
            pe.wait_ge(normed2, NCH)
            by_token = yn[:, :].rearrange("k (p j) -> k j p", j=32)
            for q in range(8):
                wait(pe, drained, q - 1)
                for j in range(4):
                    l = nc.tensor.transpose(bank(q % 2)[:, BC * j:BC * j + BC], by_token[:, 4 * q + j, :],
                                            wt("eye", 0, BC)[0:BC])
                l.then_inc(yt_turned, 1)

            pe.wait_ge(folded, 1)
            with pe.Fori(0, 2) as i:
                for j in range(2):
                    pe.wait_ge(stack_in[j], 16 * (TA + TB) * (i + 1))
                    for c in range(NCH):
                        u = 2 * NCH * i + NCH * j + c
                        n = NCH * j + c
                        pe.wait_ge(drained, 8 + u - 3)
                        a = sta[:, j, PW * 8 * c:PW * 8 * c + 8 * PW].rearrange("k (r w) -> k r w", w=PW)[:, :, 0:W]
                        b_ = stb[:, j, PW * 8 * c:PW * 8 * c + 8 * PW].rearrange("k (r w) -> k r w", w=PW)[:, :, 0:W]
                        mm(bank(n % 4)[0:127], wca[:, :], a, start=True, stop=False)
                        mm(bank(n % 4)[0:127], wcb[:, :], b_, start=False, stop=True).then_inc(conv_made, 1)

            pe.wait_ge(drained, 8 + B * NCH)
            for i in range(2):
                for u in range(4):
                    n = 4 * i + u
                    wait(pe, x2_ready, n - 3)
                    for p in range(2):
                        l = mm(bank(u)[0:BC], wt("pout", BC * p, BC * p + BC), chunk(gated[:, p, :], n),
                               start=(p == 0), stop=(p == 1))
                    l.then_inc(pout_made, 1)
                for u in range(4):
                    n = 4 * i + u
                    pe.wait_ge(x2_ready, n + 1)
                    wait(pe, h_ready, n - 3)
                    mm(bank(4 + u)[0:BC], wt("w1"), chunk(x2, n), start=True, stop=True).then_inc(w1_made, 1)

            pe.wait_ge(h_ready, NCH)

            def grapher_in(c, par):
                pe.wait_ge(xj_ready, c + 1)
                wait(pe, gg_ready, 2 * c)
                for p in range(2):
                    cols = (BC * p, BC * p + BC)
                    mm(bank(p)[0:BC], wt("wgh", *cols), chunk(h, c), start=True, stop=False)
                    l = mm(bank(p)[0:BC], wt("wgx", *cols), xj[:, par, :], start=False, stop=True)
                l.then_inc(wg_made, 1)

            def grapher_out(c, par):
                pe.wait_ge(gg_ready, 2 * (c + 1))
                wait(pe, x3_ready, c)
                for p in range(2):
                    l = mm(bank(2)[0:BC], wt("w2", BC * p, BC * p + BC), gg[:, par, p, :],
                           start=(p == 0), stop=(p == 1))
                l.then_inc(w2_made, 1)

            def mlp_in(c, par):
                pe.wait_ge(x3_ready, c + 1)
                wait(pe, gf_ready, c)
                for f in range(3):
                    l = mm(bank(3 + f), wt("wf1", 128 * f, 128 * f + 128), x3[:, par, :], start=True, stop=True)
                l.then_inc(wf1_made, 1)

            def mlp_out(c, par):
                pe.wait_ge(gf_ready, c + 1)
                wait(pe, yo_ready, c)
                for f in range(3):
                    l = mm(bank(6)[0:BC], wt("wf2", BC * f, BC * f + BC), gf[:, par, f, :],
                           start=(f == 0), stop=(f == 2))
                l.then_inc(wf2_made, 1)

            for f in range(3):
                l = mm(bank(7)[:, f:f + 1], wt("wf1", 128 * f, 128 * f + 128), col(T2), start=True, stop=True)
            l.then_inc(shift_made, 1)

            grapher_in(0, 0)
            grapher_out(0, 0)
            grapher_in(1, 1)
            mlp_in(0, 0)
            with pe.Fori(0, 3) as i:
                for u in range(2):
                    c = 2 * i + 1 + u
                    par = (1 + u) % 2
                    grapher_out(c, par)
                    mlp_out(c - 1, 1 - par)
                    grapher_in(c + 1, 1 - par)
                    mlp_in(c, par)
            grapher_out(7, 1)
            mlp_out(6, 0)
            mlp_in(7, 1)
            mlp_out(7, 1)

        @block.scalar
        def _(act):
            a = nc.scalar.activation

            def norm_chunks(i, squares, roots, gain, shift, dst, made, squared_, varied_, rooted_, scaled_, normed_):
                for u in range(4):
                    n = 4 * i + u
                    act.wait_ge(made, n + 1)
                    wait(act, varied_, n - 3)
                    a(squares[:, u, :], bank(u)[0:BC], ACT.Square).then_inc(squared_, 1)
                for u in range(4):
                    n = 4 * i + u
                    act.wait_ge(varied_, n + 1)
                    wait(act, normed_, n - 3)
                    a(roots[:, u, :], bank(4 + u)[0:BC], ACT.Sqrt, bias=vec(V_EPS)).then_inc(rooted_, 1)
                for u in range(4):
                    n = 4 * i + u
                    act.wait_ge(scaled_, n + 1)
                    a(dst(n), roots[:, u, :], ACT.Identity, bias=shift, scale=gain).then_inc(normed_, 1)

            act.wait_ge(pack_in, 16)
            for i in range(2):
                norm_chunks(i, sq, rs, vec(V_N1G), vec(V_N1B), lambda n: chunk(xn, n)[0:BC],
                            centered, squared, varied, rooted, scaled, normed)
            a(col(R1), vec(V_V1), ACT.Sqrt, bias=vec(V_BNEPS))
            a(col(R2), vec(V_V2), ACT.Sqrt, bias=vec(V_BNEPS))
            a(col(RG), wt("vecs_g", 4, 5), ACT.Sqrt, bias=vec(V_BNEPS)).then_inc(roots_ready, 1)

            def take_qk(m, par):
                act.wait_ge(q_made, m + 1)
                wait(act, stq_ready, m - 1)
                a(qs[:, par, :], bank(6), ACT.Copy, scale=wt("scales", 3, 4)).then_inc(qs_ready, 1)
                act.wait_ge(k_made, m + 1)
                wait(act, scores_made, WS * (m - 1))
                for i in range(NH):
                    base = kmv[:, par, 0, i, :]
                    dst = bass.AP(base.tensor, base.offset, [
                        base.ap[0], [2 * NH * WT, WS // 2], [NH * WT + (NH - 1 - 2 * i) * WT, 2], [1, WT]])
                    l = a(dst, bank(7).rearrange("p (w e t) -> p w e t", e=2, t=WT), ACT.Copy,
                          scale=wt("scales", i, i + 1))
                l.then_inc(kmv_ready, 1)

            def take_v(m, par):
                wait(act, mixed, 4 * (m - 1))
                for odd, made in enumerate((v0_made, v1_made)):
                    act.wait_ge(made, m + 1)
                    v = bank(6 + odd)[0:WT, 0:4 * BC].rearrange("k (x j c) -> k x j c", j=2, c=C)
                    for i in range(NH):
                        half = i ^ odd if i < 2 else odd
                        l = a(diagonal(par, odd, i // 2, half, HD * i), v[:, :, :, HD * i:HD * i + HD], ACT.Copy)
                l.then_inc(stv_ready, 1)

            def diagonal(par, odd, n, half, at):
                base = stv[64 * half:64 * half + 64, par, odd, 0, 0, n, at:at + HD]
                return bass.AP(base.tensor, base.offset, [base.ap[0], [2 * 256, 8], [256 + 32, 2], [1, HD]])

            def exps(t, pp):
                act.wait_ge(turned, t + 1)
                wait(act, mixed, t - 1)
                a(pt[:, pp, :], psum[:, 1024:1024 + 768], ACT.Exp).then_inc(probs_ready, 1)

            def attend(m, par, after=True):
                for l in range(4):
                    if after or l < 3:
                        exps(4 * m + l + 1, (l + 1) % 2)
                    if l == 0 and after:
                        take_qk(m + 1, 1 - par)
                    if l == 1 and after:
                        take_v(m + 1, 1 - par)

            act.wait_ge(zeroed, 1)
            take_qk(0, 0)
            take_v(0, 0)
            exps(0, 0)
            attend(0, 0)
            with act.Fori(0, 3) as i:
                attend(2 * i + 1, 1)
                attend(2 * i + 2, 0)
            attend(7, 1, after=False)

            for i in range(2):
                norm_chunks(i, sq2, rs2, vec(V_N2G), vec(V_N2B), lambda n: chunk(yn, n),
                            centered2, squared2, varied2, rooted2, scaled2, normed2)

            with act.Fori(0, 2) as i:
                for n in range(2 * NCH):
                    u = 2 * NCH * i + n
                    act.wait_ge(conv_made, u + 1)
                    act.wait_ge(drained, 8 + u - 3)
                    a(gel[:, n % 4, :], bank(n % 4)[0:HID], ACT.Gelu).then_inc(gelu_ready, 1)

            act.wait_ge(folded, 1)
            for i in range(2):
                for u in range(4):
                    n = 4 * i + u
                    act.wait_ge(w1_made, n + 1)
                    act.wait_ge(folded, 1)
                    a(chunk(h, n), bank(4 + u)[0:BC], ACT.Identity, bias=col(T1), scale=col(S1)).then_inc(h_ready, 1)

            def gelu_g(c, par):
                act.wait_ge(wg_made, c + 1)
                wait(act, w2_made, c - 1)
                for p in range(2):
                    a(gg[:, par, p, :], bank(p)[0:BC], ACT.Gelu, bias=col(TG), scale=col(SG)).then_inc(gg_ready, 1)

            def gelu_f(c, par):
                act.wait_ge(wf1_made, c + 1)
                wait(act, wf2_made, c - 1)
                for f in range(3):
                    l = a(gf[:, par, f, :], bank(3 + f), ACT.Gelu, bias=small[:, BF + f:BF + f + 1])
                l.then_inc(gf_ready, 1)

            gelu_g(0, 0)
            act.wait_ge(shift_ready, 1)
            def gelus(i):
                for u in range(2):
                    gelu_g(2 * i + u + 1, 1 - u)
                    gelu_f(2 * i + u, u)

            gelus(0)
            with act.Fori(1, 3) as i:
                gelus(i)
            gelu_g(7, 1)
            gelu_f(6, 0)
            gelu_f(7, 1)

        @block.vector
        def _(dve):
            v = nc.vector

            def norm_chunks(i, roots, made, rooted_, inverted_, scaled_):
                for u in range(4):
                    n = 4 * i + u
                    dve.wait_ge(rooted_, n + 1)
                    v.reciprocal(roots[:, u, :], roots[:, u, :]).then_inc(inverted_, 1)
                    dve.wait_ge(inverted_, n + 1)
                    v.tensor_tensor(roots[:, u, :], bank(u)[0:BC], roots[:, u, :], ALU.mult).then_inc(scaled_, 1)

            dve.wait_ge(pack_in, 16)
            v.tensor_copy(posr[:, :], wt("posi"))
            for odd in range(2):
                for i in range(NH):
                    at = WT * (NH - 1 - i if odd else i)
                    for p in range(2):
                        l = v.tensor_copy(biasr[0:WT, odd, p, at:at + WT], wt("rpb", WT * i, WT * i + WT))
            l.then_inc(bias_high, 1)
            dve.wait_ge(bias_high, 1)
            for odd in range(2):
                for i in range(NH):
                    at = WT * (NH - 1 - i if odd else i)
                    for p in range(2):
                        l = v.tensor_tensor(biasr[64:128, odd, p, at:at + WT], wt("rpb", WT * i, WT * i + WT),
                                            biasr[0:WT, odd, p, at:at + WT].bitcast(F32), ALU.subtract)
            l.then_inc(bias_ready, 1)
            for i in range(2):
                norm_chunks(i, rs, centered, rooted, inverted, scaled)
            dve.wait_ge(roots_ready, 1)
            v.reciprocal(small[0:BC, R1:RG + 1], small[0:BC, R1:RG + 1]).then_inc(folding, 1)
            dve.wait_ge(folding, 1)
            norms = ((S1, R1, vec(V_G1), vec(V_B1), vec(V_M1), vec(V_BE1), T1),
                     (S2, R2, vec(V_G2), vec(V_B2), vec(V_M2), vec(V_BE2), T2),
                     (SG, RG, wt("vecs_g", 1, 2), wt("vecs_g", 0, 1), wt("vecs_g", 3, 4), wt("vecs_g", 2, 3), TG))
            for s, r, gain, b0, mean, beta, t in norms:
                v.tensor_tensor(col(s), col(r), gain, ALU.mult)
                l = v.tensor_tensor(col(t), b0, mean, ALU.subtract)
            l.then_inc(folding, 1)
            dve.wait_ge(folding, 2)
            for s, r, gain, b0, mean, beta, t in norms:
                l = v.scalar_tensor_tensor(col(t), col(t), col(s), beta, ALU.mult, ALU.add)
            v.tensor_tensor(wca[:, :], wt("pin"), wt("dwa"), ALU.mult)
            v.tensor_tensor(wcb[:, :], wt("pin")[0:C * TB], wt("dwb"), ALU.mult).then_inc(folded, 1)

            def subtract_max(m, w):
                n = WS * m + w
                dve.wait_ge(scores_made, n + 1)
                s = bank(w % 2, 2 * NH * WT).rearrange("p (g k) -> p g k", k=WT)
                v.tensor_reduce(mx[:, w % 2, :], s, AX.X, ALU.max).then_inc(max_ready, 1)
                dve.wait_ge(max_ready, n + 1)
                wait(dve, turned, 4 * m + w // 2 - 1)
                dst = diff[:, (w // 2) % 2, :, NH * WT * (w % 2):NH * WT * (w % 2 + 1)]
                v.tensor_tensor(dst.rearrange("p i (h k) -> p i h k", k=WT), s.rearrange("p (i h) k -> p i h k", i=2),
                                mx[:, w % 2, :].rearrange("p (i h) -> p i h", i=2).unsqueeze(3)
                                .to_broadcast([128, 2, NH, WT]), ALU.subtract).then_inc(diff_ready, 1)

            def divide(m, par):
                g = 2 * m + par
                dve.wait_ge(mixed, 2 * g + 2)
                o = bank(4 + par)
                v.reciprocal(rz[:, par, :], o[64:128]).then_inc(rz_ready, 1)
                dve.wait_ge(rz_ready, g + 1)
                wait(dve, projected, m)
                v.tensor_tensor(on[0:64, par, :], o[0:64], rz[:, par, :], ALU.mult).then_inc(on_ready, 1)

            def residual(m):
                dve.wait_ge(projected, m + 1)
                src = bank(6)[0:BC].rearrange("p (w r s) -> p w r s", r=WS, s=WS)
                add = chunk(xin, m).rearrange("p (w r s) -> p w r s", r=WS, s=WS)
                dst = x1[:, bass.ds(SHIFT + WS * m, WS), SHIFT:SHIFT + W].rearrange("p r (w s) -> p w r s", s=WS)
                v.tensor_tensor(dst, src, add, ALU.add).then_inc(x1_ready, 1)

            def attend(m, par, before=True, after=True, copy=True):
                for l in range(4):
                    if l == 3 and copy:
                        copy_xs(m + 2, par)
                    if l == 0 and before:
                        divide(m - 1, 1)
                    if l == 2:
                        divide(m, 0)
                    if l == 3 and before:
                        residual(m - 1)
                    if after or l < 2:
                        for e in range(2):
                            if l < 2:
                                subtract_max(m, 2 * l + 4 + e)
                            else:
                                subtract_max(m + 1, 2 * l - 4 + e)

            def copy_xs(m, par):
                wait(dve, v1_made, m - 1)
                v.tensor_copy(xs[:, par, :], chunk(xn, m)).then_inc(xs_ready, 1)

            dve.wait_ge(feat_in, 16)
            dve.wait_ge(normed, NCH)
            copy_xs(0, 0)
            copy_xs(1, 1)
            for w in range(4):
                subtract_max(0, w)
            attend(0, 0, before=False)
            with dve.Fori(0, 2) as i:
                attend(2 * i + 1, 1)
                attend(2 * i + 2, 0)
            attend(5, 1)
            attend(6, 0, copy=False)
            attend(7, 1, after=False, copy=False)
            divide(7, 1)
            residual(7)
            dve.wait_ge(x1_ready, NCH)
            v.tensor_copy(x1[:, SHIFT:XP, 0:SHIFT], x1[:, SHIFT:XP, W:XP]).then_inc(wrapped_right, 1)
            dve.wait_ge(wrapped_right, 1)
            v.tensor_copy(x1[:, 0:SHIFT, 0:W], x1[:, H:XP, 0:W]).then_inc(wrap_ready, 1)

            for i in range(2):
                norm_chunks(i, rs2, centered2, rooted2, inverted2, scaled2)
            for q in range(8):
                dve.wait_ge(yt_turned, q + 1)
                v.tensor_copy(yt[:, :, 4 * q:4 * q + 4, :].rearrange("p b j c -> p j b c"),
                              bank(q % 2)[:, 0:4 * BC].rearrange("p (j b c) -> p j b c", b=B, c=C))\
                    .then_inc(drained, 1)

            dve.wait_ge(pad_zero, 2)
            with dve.Fori(0, 2) as i:
                for n in range(2 * NCH):
                    j, c = divmod(n, NCH)
                    dve.wait_ge(gelu_ready, 2 * NCH * i + n + 1)
                    v.tensor_tensor(gated[64 * j:64 * j + HID, bass.ds(i, 1), c * CH:(c + 1) * CH],
                                    bank(n % 4)[64:64 + HID].unsqueeze(1), gel[:, n % 4, :].unsqueeze(1),
                                    ALU.mult).then_inc(drained, 1)

            for i in range(2):
                for u in range(4):
                    n = 4 * i + u
                    dve.wait_ge(pout_made, n + 1)
                    v.tensor_tensor(chunk(x2, n).rearrange("p (r w) -> p r w", w=W),
                                    bank(u)[0:BC].rearrange("p (r w) -> p r w", w=W), rows8(x1, n), ALU.add)\
                        .then_inc(x2_ready, 1)
            dve.wait_ge(h_ready, NCH)
            v.tensor_reduce(hmin[:, :, :], h[:, :].rearrange("p (r q w) -> p q w r", q=2, w=W), AX.X, ALU.min)
            v.tensor_reduce(wmin[:, :, :], h[:, :].rearrange("p (r x q) -> p r q x", q=2, x=W // 2),
                            AX.X, ALU.min).then_inc(hmin_ready, 1)
            dve.wait_ge(hmin_ready, 1)
            dve.wait_ge(shift_made, 1)
            v.tensor_tensor(small[:, BF:BF + 3], bank(7)[:, 0:3], wt("bf1"), ALU.add).then_inc(shift_ready, 1)

            def nearest(c, par):
                wait(dve, xj_ready, c - 1)
                for q in range(2):
                    wm = wmin[:, bass.ts(c, 8), :].rearrange("p (r q) x -> p q r x", q=2)[:, q]
                    v.tensor_tensor(near[:, par].rearrange("p (r q) (w x) -> p q r w x", q=2, x=2)[:, q],
                                    hmin[:, q, :].rearrange("p (w x) -> p w x", x=2).unsqueeze(1)
                                    .to_broadcast([BC, 4, W // 2, 2]),
                                    wm.unsqueeze(2).to_broadcast([BC, 4, W // 2, 2]), ALU.min)\
                        .then_inc(near_ready, 1)

            def add_shortcut(c, par):
                dve.wait_ge(w2_made, c + 1)
                wait(dve, wf1_made, c - 1)
                v.scalar_tensor_tensor(x3[:, par, :], bank(2)[0:BC], col(S2), chunk(x2, c), ALU.mult, ALU.add)\
                    .then_inc(x3_ready, 1)

            def finish(i, par):
                dve.wait_ge(wf2_made, 2 * i + par + 1)
                wait(dve, stored[par], 16 * i)
                v.tensor_scalar(yo[:, par, :], bank(6)[0:BC], vec(V_BF2), None, ALU.add).then_inc(yo_ready, 1)

            nearest(0, 0)
            nearest(1, 1)
            add_shortcut(0, 0)
            def two_chunks(i):
                for u in range(2):
                    c, par = 2 * i + 1 + u, 1 - u
                    add_shortcut(c, par)
                    nearest(c + 1, 1 - par)
                    finish(i, u)

            two_chunks(0)
            with dve.Fori(1, 3) as i:
                two_chunks(i)
            add_shortcut(7, 1)
            finish(3, 0)
            finish(3, 1)
    return nc


def lay_out(a):
    import numpy as np

    f = np.float32
    img, half = np.arange(B), np.arange(2)

    def blocks(w, rows=None, cols=None):
        o, n = w.shape
        m = np.zeros((B * n, B * o), f)
        for b in range(B):
            m[n * b:n * b + n, o * b:o * b + o] = w.T
        return m

    x = np.roll(a["x"], (-SHIFT, -SHIFT), axis=(2, 3))
    x = x.reshape(BC, H // WS, WS, W // WS, WS).transpose(0, 1, 3, 2, 4).reshape(BC, NT)

    last_row = np.arange(H) >= H - SHIFT
    last_col = np.arange(W) >= W - SHIFT
    region = (2 * last_row[:, None] + last_col[None, :]).reshape(H // WS, WS, W // WS, WS)
    region = region.transpose(0, 2, 1, 3).reshape(NT)
    feat = np.zeros((1 + NREG, NT), f)
    feat[0] = 1.0
    for r in range(NREG):
        feat[1 + r] = region == r

    qkv_w, qkv_b = a["L0_conv_qkv_w"], a["L0_conv_qkv_b"]
    p = {n: np.zeros(shape, f) for n, shape in PACK.items()}
    for b in range(B):
        rows = slice(C * b, C * b + C)
        p["wq"][rows, 32 * b:32 * b + C] = qkv_w[0:C].T
        p["wk"][rows, 32 * b:32 * b + C] = qkv_w[C:2 * C].T
        p["wv"][rows, rows] = qkv_w[2 * C:].T
        p["wq"][BC, 32 * b:32 * b + C] = qkv_b[0:C]
        p["wk"][BC, 32 * b:32 * b + C] = qkv_b[C:2 * C]
        p["wv"][BC, rows] = qkv_b[2 * C:]
        for r in range(NREG):
            p["wq"][BC + 1 + r, 32 * b + C + r] = 1.0
            p["wk"][BC, 32 * b + C + r] = MASKED
            p["wk"][BC + 1 + r, 32 * b + C + r] = -MASKED
            p["scales"][32 * b + C + r, :] = 1.0
        for i in range(NH):
            p["scales"][32 * b + HD * i:32 * b + HD * i + HD, i] = 1.0
        p["scales"][32 * b:32 * b + C, 3] = HD ** -0.5
        pair, j = divmod(b, 2)
        p["wproj"][32 * j:32 * j + C, BC * pair + C * b:BC * pair + C * b + C] = a["L0_conv_proj_w"].T
        p["wproj"][64, C * b:C * b + C] = a["L0_conv_proj_b"]
        p["pout"][64 * j:64 * j + HID, BC * pair + C * b:BC * pair + C * b + C] = a["L0_conv_pout_w"].T
        cols = slice(BC * pair + G2 * j, BC * pair + G2 * j + G2)
        p["wgh"][rows, cols] = a["L1_conv_wg"][:, 0:C].T
        p["wgx"][rows, cols] = a["L1_conv_wg"][:, C:].T
        p["w2"][G2 * j:G2 * j + G2, BC * pair + C * b:BC * pair + C * b + C] = a["L1_conv_w2"].T
        p["wf1"][rows, F4 * b:F4 * b + F4] = a["L1_conv_wf1"].T
        p["center"][rows, rows] = -1.0 / C
        p["avg"][rows, rows] = 1.0 / C
    p["center"][np.arange(BC), np.arange(BC)] = 1.0 - 1.0 / C
    y, z = np.divmod(np.arange(WT), WS)
    at = (y[:, None] - y[None, :] + WS - 1) * (2 * WS - 1) + z[:, None] - z[None, :] + WS - 1
    p["rpb"][:] = a["L0_conv_rpb_table"][at].transpose(0, 2, 1).reshape(WT, NH * WT)
    p["posi"][:] = np.tile(np.eye(WT, dtype=f), (2, 2))
    p["eye"][:] = np.eye(128, dtype=f)
    per_channel = ["L0_conv_norm1_g", "L0_conv_norm1_b", "L0_conv_norm2_g", "L0_conv_norm2_b", "L1_conv_b1",
                   "L1_conv_g1", "L1_conv_be1", "L1_conv_m1", "L1_conv_v1", "L1_conv_b2", "L1_conv_g2",
                   "L1_conv_be2", "L1_conv_m2", "L1_conv_v2", "L1_conv_bf2"]
    for n, name in enumerate(per_channel):
        p["vecs"][:, n] = np.tile(a[name], B)
    p["vecs"][:, V_EPS] = LN_EPS
    p["vecs"][:, V_BNEPS] = BN_EPS
    for n, name in enumerate(["bg", "gg", "beg", "mg", "vg"]):
        p["vecs_g"][:, n] = np.tile(a["L1_conv_" + name], 2)
    p["bf1"][:] = np.tile(a["L1_conv_bf1"], B).reshape(3, 128).T
    pin, taps = a["L0_conv_pin_w"], a["L0_conv_dw_w"].reshape(2 * HID, 9)
    for part in range(2):
        outs, src = slice(64 * part, 64 * part + HID), slice(HID * part, HID * part + HID)
        for t in range(TA + TB):
            name, k = ("dwa", t) if t < TA else ("dwb", t - TA)
            if t < TA:
                p["pin"][C * t:C * t + C, outs] = pin[src].T
            p[name][C * k:C * k + C, outs] = taps[None, src, t]
    p["w1"][:] = blocks(a["L1_conv_w1"])
    p["wf2"][:] = blocks(a["L1_conv_wf2"]).reshape(3, 128, BC).transpose(1, 0, 2).reshape(128, 3 * BC)
    pack = np.zeros((128, PACK_W), f)
    for n, (r, c) in PACK.items():
        pack[0:r, PACK_AT[n]:PACK_AT[n] + c] = p[n]
    return {"xw": np.ascontiguousarray(x), "feat": feat, "pack": pack}


def kernel(**inputs):
    import numpy as np
    import concourse.bacc as bacc
    from concourse.bass_utils import run_bass_kernel_spmd

    arrays = lay_out({name: np.asarray(value) for name, value in inputs.items()})
    nc = bacc.Bacc("TRN2", target_bir_lowering=False, num_devices=1)
    args = [nc.dram_tensor(n, v.shape, F32, kind="ExternalInput").ap() for n, v in arrays.items()]
    out = nc.dram_tensor("out", (B, C, H, W), F32, kind="ExternalOutput").ap()
    build(nc, *args, out)
    return run_bass_kernel_spmd(nc, [arrays], core_ids=[0]).results[0]["out"]
```

```python
from contextlib import ExitStack

import concourse.bass as bass
from concourse import mybir

F32 = mybir.dt.float32
F32R = mybir.dt.float32r
ALU = mybir.AluOpType
ACT = mybir.ActivationFunctionType
AX = mybir.AxisListType

B, C, H, W = 4, 24, 64, 64
NT = H * W
WS, SHIFT = 8, 4
NH, HD = 3, 8
HID = 63
BC = B * C
G2 = 2 * C
F4 = 4 * C
CH = 512
NCH = NT // CH
WT = WS * WS
NREG = 4
KX = BC + 1 + NREG
TOK = CH // 128
GR = TOK * B
TA, TB = 5, 4
MASKED = -100.0
LN_EPS, BN_EPS = 1e-5, 1e-5

PACK = {
    "wq": (KX, 128), "wk": (KX, 128), "wv": (KX, BC), "scales": (128, 4),
    "rpb": (WT, NH * WT), "posi": (128, 128), "eye": (128, 128),
    "wproj": (BC + 1, 4 * BC), "vecs": (BC, 15), "gain2": (128, C), "shift2": (128, C), "edge": (C * TA, 4),
    "vecs_g": (BC, 5), "bf1": (128, 3), "pin": (C * TA, 127), "dwa": (C * TA, 127), "dwb": (C * TB, 127),
    "pout": (128, 2 * BC), "w1": (BC, BC), "wgh": (BC, 2 * BC), "wgx": (BC, 2 * BC),
    "w2": (BC, 2 * BC), "wf1": (BC, B * F4), "wf2": (128, 3 * BC),
}
PACK_AT, _at = {}, 0
for _name, (_r, _c) in PACK.items():
    PACK_AT[_name] = _at
    _at += _c
PACK_W = _at
(V_N1G, V_N1B, V_B1, V_G1, V_BE1, V_M1, V_V1, V_B2, V_G2, V_BE2, V_M2, V_V2, V_BF2, V_BNEPS) = range(14)
PLACES = (((0, 0), (0, 1)), ((0, 2), (1, 2)), ((1, 1), (1, 0)))
VW = 2 * 2 * HD + 2


def build(nc, xw, xt, feat, pack, out):
    scratch = nc.dram_tensor("scratch", [B, C * NT], F32, kind="Internal").ap()

    with ExitStack() as ctx:
        def sb(stack, name, shape, dt=F32):
            return stack.enter_context(nc.sbuf_tensor(name, shape, dt))

        def sem(name):
            return ctx.enter_context(nc.semaphore(name))

        psum = ctx.enter_context(nc.psum_tensor("psum", [128, 8 * 512], F32))

        def bank(n, cols=512):
            return psum[:, 512 * n:512 * n + cols]

        pk = sb(ctx, "pk", [128, PACK_W])
        x1 = sb(ctx, "x1", [BC, H, W])
        small = sb(ctx, "small", [128, 16])
        wca = sb(ctx, "wca", [C * TA, 127])
        wcb = sb(ctx, "wcb", [C * TB, 127])
        sta = sb(ctx, "sta", [C * TA, 2, NT])
        stb = sb(ctx, "stb", [C * TB, 2, NT])

        def wt(name, c0=0, c1=None):
            r, c = PACK[name]
            a = PACK_AT[name]
            return pk[0:r, a + c0:a + (c if c1 is None else c1)]

        def vec(n):
            return wt("vecs", n, n + 1)

        att = ExitStack()
        xin = sb(att, "xin", [KX, NT])
        xtok = sb(att, "xtok", [128, NCH, GR * C])
        biasr = sb(att, "biasr", [128, 2, 2, NH * WT], F32R)
        posr = sb(att, "posr", [128, 128], F32R)
        cen = sb(att, "cen", [128, 2, GR, C])
        cen2 = sb(att, "cen2", [128, 2, GR, C])
        sqr = sb(att, "sqr", [128, 2, GR, C])
        sums = sb(att, "sums", [128, 2, GR])
        squares = sb(att, "squares", [128, 2, GR])
        var = sb(att, "var", [128, 2, GR])
        rstd = sb(att, "rstd", [128, 2, GR])
        power = sb(att, "power", [128, GR])
        xhat = sb(att, "xhat", [128, TOK, BC])
        gained = sb(att, "gained", [128, GR, C])
        ytok = sb(att, "ytok", [128, 2, GR, C])
        xs = sb(att, "xs", [KX, 2, CH])
        stq = sb(att, "stq", [128, 2, 2, WS, 128])
        kmv = sb(att, "kmv", [128, 2, WS, NH, WT])
        val = sb(att, "val", [128, 2, WS // 2, 2, 3, VW])
        diff = sb(att, "diff", [128, 2, 2, 2 * NH * WT])
        mx = sb(att, "mx", [128, 2, 2 * NH])
        pt = sb(att, "pt", [128, 2, 768])
        rz = sb(att, "rz", [128, 2, 12, 2])
        ot = sb(att, "ot", [128, 2, 12, 16])
        mt = sb(att, "mt", [BC + 1, CH])
        x1s = sb(att, "x1s", [BC, 2, 8, W])
        att.close()

        late = ExitStack()
        gated = sb(late, "gated", [128, 2, NT])
        gel = sb(late, "gel", [HID, 4, CH])
        late.close()
        last = ExitStack()
        _gated = sb(last, "gated_below", [128, 2, NT])
        x2 = sb(last, "x2", [BC, NT])
        h = sb(last, "h", [BC, NT])
        hmin = sb(last, "hmin", [BC, 2, W])
        hpart = sb(last, "hpart", [BC, 2, 2, W])
        wmin = sb(last, "wmin", [BC, H, 2])
        near = sb(last, "near", [BC, 2, 8, W])
        xj = sb(last, "xj", [BC, 2, CH])
        gg = sb(last, "gg", [BC, 2, 2, CH])
        x3 = sb(last, "x3", [BC, 2, CH])
        gf = sb(last, "gf", [128, 2, 3, CH])
        yo = sb(last, "yo", [BC, 2, CH])
        last.close()

        pack_in, x_in, feat_in = sem("pack_in"), sem("x_in"), sem("feat_in")
        zeroed = sem("zeroed")
        bias_high, bias_ready = sem("bias_high"), sem("bias_ready")
        roots_ready, folding, folded = sem("roots_ready"), sem("folding"), sem("folded")
        shift_made, shift_ready = sem("shift_made"), sem("shift_ready")
        sum_ready, cen_ready, sqr_ready, ssq_ready, var_ready, rstd_ready, xhat_ready, xs_turned, xs_ready = (
            sem(n) for n in ("sum_ready", "cen_ready", "sqr_ready", "ssq_ready", "var_ready", "rstd_ready",
                             "xhat_ready", "xs_turned", "xs_ready"))
        rows_ready = sem("rows_ready")
        x1_turned, sum2_ready, cen2_ready, sqr2_ready, ssq2_ready, var2_ready, rstd2_ready = (
            sem(n) for n in ("x1_turned", "sum2_ready", "cen2_ready", "sqr2_ready", "ssq2_ready", "var2_ready",
                             "rstd2_ready"))
        gained_ready, norm2_ready, y_ready = sem("gained_ready"), sem("norm2_ready"), sem("y_ready")
        y_stored = [sem(f"y_stored{par}") for par in range(2)]
        q_made, k_made, stq_ready, kmv_ready = (sem(n) for n in ("q_made", "k_made", "stq_ready", "kmv_ready"))
        v0_made, v1_made, val_ready = sem("v0_made"), sem("v1_made"), sem("val_ready")
        scores_made, max_ready, diff_ready, turned, probs_ready, mixed = (
            sem(n) for n in ("scores_made", "max_ready", "diff_ready", "turned", "probs_ready", "mixed"))
        rz_ready, ot_ready, out_turned, mt_ready, projected, x1s_ready, x1_ready = (
            sem(n) for n in ("rz_ready", "ot_ready", "out_turned", "mt_ready", "projected", "x1s_ready", "x1_ready"))
        borders, stack_in, edged = sem("borders"), [sem(f"stack_in{j}") for j in range(2)], sem("edged")
        conv_made, gelu_ready, gated_ready = sem("conv_made"), sem("gelu_ready"), sem("gated_ready")
        pout_made, x2_ready, w1_made, h_ready = sem("pout_made"), sem("x2_ready"), sem("w1_made"), sem("h_ready")
        hpart_ready, hmin_ready = sem("hpart_ready"), sem("hmin_ready")
        near_ready, xj_ready, wg_made, gg_ready = (
            sem(n) for n in ("near_ready", "xj_ready", "wg_made", "gg_ready"))
        w2_made, x3_ready, wf1_made, gf_ready, wf2_made, yo_ready = (
            sem(n) for n in ("w2_made", "x3_ready", "wf1_made", "gf_ready", "wf2_made", "yo_ready"))
        stored = [sem(f"stored{par}") for par in range(2)]

        S1, T1, S2, T2, SG, TG, BF = 0, 1, 2, 3, 4, 5, 6
        R1, R2, RG = 9, 10, 11

        def col(n, rows=BC):
            return small[0:rows, n:n + 1]

        def wait(eng, s, count):
            if isinstance(count, int) and count <= 0:
                return
            eng.wait_ge(s, count)

        def chunk(buf, n):
            return buf[:, bass.ts(n, CH)]

        def tap_range(t):
            off = (t // 3 - 1) * W + t % 3 - 1
            return max(0, -off), max(0, off), NT - abs(off)

        block = ctx.enter_context(nc.Block())

        @block.sync
        def _(sp):
            sp.dma_start(xtok[:, :, :].rearrange("p m n -> p (m n)"), xt).then_inc(x_in, 16)
            sp.dma_start(pk[:, :], pack).then_inc(pack_in, 16)
            sp.dma_start(xin[BC:KX, :], feat).then_inc(feat_in, 16)
            sp.dma_start(xin[0:BC, :], xw).then_inc(feat_in, 16)

            def store_y(m, par):
                sp.wait_ge(y_ready, m + 1)
                at = (8 * m + SHIFT) * W
                parts = [(0, TOK, at)]
                if isinstance(m, int) and m == NCH - 1:
                    parts = [(0, TOK // 2, at), (TOK // 2, TOK // 2, 0)]
                for k0, k, token in parts:
                    for b in range(B):
                        dst = scratch[b].rearrange("(t c) -> t c", c=C)[bass.ds(token, 128 * k), :]
                        sp.dma_start(dst.rearrange("(k p) c -> p k c", p=128),
                                     ytok[:, par].rearrange("p (k b) c -> p k b c", b=B)[:, k0:k0 + k, b, :])\
                            .then_inc(y_stored[par], 16)

            store_y(0, 0)
            store_y(1, 1)
            with sp.Fori(1, 3) as i:
                store_y(2 * i, 0)
                store_y(2 * i + 1, 1)
            store_y(6, 0)
            store_y(7, 1)
            sp.wait_ge(borders, 1)
            sp.wait_ge(y_stored[0], 16 * B * 5)
            sp.wait_ge(y_stored[1], 16 * B * 6)
            for b in range(B):
                if b >= 2:
                    sp.wait_ge(conv_made, NCH * (b - 1))
                src = scratch[b].rearrange("(c n) -> c n", c=C)
                for t in range(TA + TB):
                    stack, k = (sta, t) if t < TA else (stb, t - TA)
                    d0, s0, n = tap_range(t)
                    sp.dma_start(stack[C * k:C * k + C, b % 2, d0:d0 + n], src[:, s0:s0 + n])\
                        .then_inc(stack_in[b % 2], 16)
            out_rows = out.rearrange("b c h w -> (b c) (h w)")
            for c in range(NCH):
                sp.wait_ge(yo_ready, c + 1)
                sp.dma_start(out_rows[:, c * CH:(c + 1) * CH], yo[:, c % 2, :]).then_inc(stored[c % 2], 16)
            for par in range(2):
                sp.wait_ge(stored[par], 16 * NCH // 2)

        @block.gpsimd
        def _(pool):
            g = nc.gpsimd
            g.memset(stq[:], 0.0)
            g.memset(power[:], -0.5).then_inc(y_stored[0], 16 * B)
            g.memset(mt[:], 1.0).then_inc(y_stored[1], 16 * B)
            g.memset(val[:], 0.0).then_inc(zeroed, 1)
            pool.wait_ge(zeroed, 1)
            blocks = val[:, :, :, :, :, :].rearrange("k a t p n c -> k (a t p n) c")
            for x in range(2):
                l = g.memset(blocks[64 * x:64 * x + 64, :, 2 * 2 * HD + x:2 * 2 * HD + x + 1], 1.0)
            l.then_inc(zeroed, 1)
            pool.wait_ge(zeroed, 2)
            for stack in (sta, stb):
                g.memset(stack[:, :, 0:W + 1], 0.0)
                l = g.memset(stack[:, :, NT - W - 1:NT], 0.0)
            l.then_inc(borders, 1)

            def root(k, n, varied, done):
                pool.wait_ge(varied, n)
                g.tensor_tensor(rstd[:, k, :], var[:, k, :], power[:, :], ALU.pow).then_inc(done, 1)

            def second_norm(i, par):
                m = 2 * i + par
                pool.wait_ge(cen2_ready, m + 1)
                g.tensor_tensor(gained[:, :, :], cen2[:, par],
                                wt("gain2").unsqueeze(1).to_broadcast([128, GR, C]), ALU.mult)\
                    .then_inc(gained_ready, 1)
                root(1, m + 1, var2_ready, rstd2_ready)
                pool.wait_ge(norm2_ready, m + 1)
                pool.wait_ge(y_stored[par], 16 * B * (i + 1))
                g.tensor_tensor(ytok[:, par], cen2[:, par],
                                wt("shift2").unsqueeze(1).to_broadcast([128, GR, C]), ALU.add)\
                    .then_inc(y_ready, 1)

            def keep_x1(m, par):
                pool.wait_ge(x1s_ready, m + 1)
                r0 = 8 * m + SHIFT
                if isinstance(m, int) and m == NCH - 1:
                    g.tensor_copy(x1[:, r0:H, :], x1s[:, par, 0:H - r0])
                    g.tensor_copy(x1[:, 0:SHIFT, :], x1s[:, par, H - r0:8]).then_inc(x1_ready, 1)
                else:
                    g.tensor_copy(x1[:, bass.ds(r0, 8), :], x1s[:, par]).then_inc(x1_ready, 1)

            root(0, 1, var_ready, rstd_ready)
            root(0, 2, var_ready, rstd_ready)

            def step(i, par, first=True, before=True, second=True):
                m = 2 * i + par
                if first:
                    root(0, m + 3, var_ready, rstd_ready)
                if second:
                    second_norm(i - 1, par)
                if before:
                    keep_x1(m - 1, 1 - par)

            step(0, 0, before=False, second=False)
            step(0, 1, second=False)
            with pool.Fori(1, 3) as i:
                step(i, 0)
                step(i, 1)
            step(3, 0, first=False)
            step(3, 1, first=False)
            second_norm(3, 0)
            keep_x1(7, 1)
            second_norm(3, 1)
            def sub_near(c, par):
                pool.wait_ge(near_ready, 2 * (c + 1))
                wait(pool, wg_made, c - 1)
                g.tensor_tensor(xj[:, par, :], chunk(h, c), near[:, par].rearrange("p r w -> p (r w)"),
                                ALU.subtract).then_inc(xj_ready, 1)

            sub_near(0, 0)
            sub_near(1, 1)
            with pool.Fori(1, 4) as i:
                for u in range(2):
                    sub_near(2 * i + u, u)

        @block.tensor
        def _(pe):
            mm = nc.tensor.matmul

            def make_qk(m, par):
                pe.wait_ge(xs_ready, m + 1)
                wait(pe, rows_ready, m + 1)
                wait(pe, x1s_ready, m - 2)
                mm(bank(6), wt("wq"), xs[:, par, :], start=True, stop=True).then_inc(q_made, 1)
                mm(bank(7), wt("wk"), xs[:, par, :], start=True, stop=True).then_inc(k_made, 1)

            def make_v(m, par):
                for odd, (free, made) in enumerate(((stq_ready, v0_made), (kmv_ready, v1_made))):
                    pe.wait_ge(free, m + 1)
                    for w in range(WS // 2):
                        t0 = (2 * w + odd) * WT
                        l = mm(bank(6 + odd)[0:WT, BC * w:BC * w + BC], xs[:, par, t0:t0 + WT], wt("wv"),
                               start=True, stop=True)
                    l.then_inc(made, 1)

            def turn_xhat(m):
                pe.wait_ge(xhat_ready, m + 1)
                for k in range(TOK):
                    l = nc.tensor.transpose(bank(7)[0:BC, 128 * k:128 * k + 128], xhat[:, k, :], wt("eye"))
                l.then_inc(xs_turned, 1)

            def turn_x1(m, par):
                pe.wait_ge(x1s_ready, m + 1)
                rows = x1s[:, par].rearrange("k r w -> k (r w)")
                for k in range(TOK):
                    l = nc.tensor.transpose(bank(7)[:, BC * k:BC * k + BC], rows[:, 128 * k:128 * k + 128],
                                            wt("eye", 0, BC)[0:BC])
                l.then_inc(x1_turned, 1)

            def scores(m, w, par):
                n = WS * m + w
                if w == 0:
                    pe.wait_ge(stq_ready, m + 1)
                    pe.wait_ge(kmv_ready, m + 1)
                wait(pe, diff_ready, n - 1)
                s = bank(w % 2, 2 * NH * WT)
                mm(s, posr[:, :], biasr[:, w % 2].rearrange("k p n -> k (p n)"), start=True, stop=True)
                for p in range(2):
                    l = mm(s[:, NH * WT * p:NH * WT * (p + 1)], stq[:, par, p, w, :],
                           kmv[:, par, w, :, :].rearrange("k h n -> k (h n)"), start=False, stop=True,
                           skip_group_check=True)
                l.then_inc(scores_made, 1)

            def turn(t, w0):
                pe.wait_ge(diff_ready, 2 * (t + 1))
                wait(pe, probs_ready, t)
                for p in range(2):
                    for k in range(3):
                        at = 384 * p + 128 * k
                        l = nc.tensor.transpose(psum[:, 1024 + at:1024 + at + 128],
                                                diff[:, (w0 // 2) % 2, p, 128 * k:128 * k + 128], wt("eye"))
                l.then_inc(turned, 1)

            def mix(m, l, par):
                t = 4 * m + l
                if l == 0:
                    pe.wait_ge(val_ready, m + 1)
                if l % 2 == 0:
                    wait(pe, ot_ready, 2 * m + l // 2 - 1)
                pe.wait_ge(probs_ready, t + 1)
                o = bank(4 + l // 2)
                for p in range(2):
                    for k in range(3):
                        at, src = VW * (6 * (l % 2) + 3 * p + k), 384 * p + 128 * k
                        x = mm(o[:, at:at + VW], pt[:, l % 2, src:src + 128], val[:, par, l, p, k, :],
                               start=True, stop=True)
                x.then_inc(mixed, 1)

            def turn_out(m):
                pe.wait_ge(ot_ready, 2 * m + 2)
                flat = ot[:, :, :, :].rearrange("k a n c -> k (a n c)")
                for k in range(4):
                    l = nc.tensor.transpose(bank(6)[0:BC, 128 * k:128 * k + 128], flat[:, BC * k:BC * k + BC],
                                            wt("eye"))
                l.then_inc(out_turned, 1)

            def project(m):
                pe.wait_ge(mt_ready, m + 1)
                src = mt[:, :].rearrange("k (t j q) -> k j t q", j=2, q=WT)
                dst = bank(6)[0:BC].rearrange("k (t e q) -> k e t q", e=2, q=WT)
                for e in range(2):
                    for j in range(2):
                        at = BC * (2 * e + j)
                        l = mm(dst[:, e], wt("wproj", at, at + BC), src[:, j], start=(j == 0), stop=(j == 1))
                l.then_inc(projected, 1)

            def attend(m, par, coming=True, after=True, before=True, second=True):
                for l in range(4):
                    t = 4 * m + l
                    if after or l < 3:
                        turn(t + 1, (2 * l + 2) % WS)
                    if after or l < 2:
                        for e in range(2):
                            if l < 2:
                                scores(m, 2 * l + 4 + e, par)
                            else:
                                scores(m + 1, 2 * l - 4 + e, 1 - par)
                    if l == 0 and after:
                        make_qk(m + 1, 1 - par)
                    if l == 1 and after:
                        make_v(m + 1, 1 - par)
                    if l == 2:
                        pe.wait_ge(val_ready, m + 2 if after else m + 1)
                        if before:
                            turn_out(m - 1)
                        if second:
                            turn_x1(m - 2, par)
                    if l == 3:
                        if coming:
                            if second:
                                pe.wait_ge(cen2_ready, m - 1)
                            turn_xhat(m + 2)
                        if before:
                            project(m - 1)
                    mix(m, l, par)

            pe.wait_ge(pack_in, 16)
            turn_xhat(0)
            pe.wait_ge(xs_ready, 1)
            turn_xhat(1)
            pe.wait_ge(xs_ready, 2)
            pe.wait_ge(zeroed, 2)
            make_qk(0, 0)
            make_v(0, 0)
            pe.wait_ge(bias_ready, 1)
            scores(0, 0, 0)
            scores(0, 1, 0)
            turn(0, 0)
            scores(0, 2, 0)
            scores(0, 3, 0)
            attend(0, 0, before=False, second=False)
            attend(1, 1, second=False)
            with pe.Fori(1, 3) as i:
                attend(2 * i, 0)
                attend(2 * i + 1, 1)
            attend(6, 0, coming=False)
            attend(7, 1, coming=False, after=False)
            pe.wait_ge(cen2_ready, 6)
            pe.wait_ge(x1s_ready, 7)
            turn_x1(6, 0)
            turn_out(7)
            project(7)
            pe.wait_ge(cen2_ready, 7)
            turn_x1(7, 1)

            pe.wait_ge(folded, 1)
            pe.wait_ge(cen2_ready, 8)
            for b in range(B):
                pe.wait_ge(edged, b + 1)
                for c in range(NCH):
                    u = NCH * b + c
                    wait(pe, gated_ready, u - 3)
                    mm(bank(u % 4)[0:127], wca[:, :], chunk(sta[:, b % 2], c), start=True, stop=False)
                    mm(bank(u % 4)[0:127], wcb[:, :], chunk(stb[:, b % 2], c), start=False, stop=True)\
                        .then_inc(conv_made, 1)

            pe.wait_ge(gated_ready, B * NCH)
            for i in range(2):
                for u in range(4):
                    n = 4 * i + u
                    wait(pe, x2_ready, n - 3)
                    for p in range(2):
                        l = mm(bank(u)[0:BC], wt("pout", BC * p, BC * p + BC), chunk(gated[:, p, :], n),
                               start=(p == 0), stop=(p == 1))
                    l.then_inc(pout_made, 1)
                for u in range(4):
                    n = 4 * i + u
                    pe.wait_ge(x2_ready, n + 1)
                    wait(pe, h_ready, n - 3)
                    mm(bank(4 + u)[0:BC], wt("w1"), chunk(x2, n), start=True, stop=True).then_inc(w1_made, 1)

            pe.wait_ge(h_ready, NCH)

            def grapher_in(c, par):
                pe.wait_ge(xj_ready, c + 1)
                wait(pe, gg_ready, 2 * c)
                for p in range(2):
                    cols = (BC * p, BC * p + BC)
                    mm(bank(p)[0:BC], wt("wgh", *cols), chunk(h, c), start=True, stop=False)
                    l = mm(bank(p)[0:BC], wt("wgx", *cols), xj[:, par, :], start=False, stop=True)
                l.then_inc(wg_made, 1)

            def grapher_out(c, par):
                pe.wait_ge(gg_ready, 2 * (c + 1))
                wait(pe, x3_ready, c)
                for p in range(2):
                    l = mm(bank(2)[0:BC], wt("w2", BC * p, BC * p + BC), gg[:, par, p, :],
                           start=(p == 0), stop=(p == 1))
                l.then_inc(w2_made, 1)

            def mlp_in(c, par):
                pe.wait_ge(x3_ready, c + 1)
                wait(pe, gf_ready, c)
                for f in range(3):
                    l = mm(bank(3 + f), wt("wf1", 128 * f, 128 * f + 128), x3[:, par, :], start=True, stop=True)
                l.then_inc(wf1_made, 1)

            def mlp_out(c, par):
                pe.wait_ge(gf_ready, c + 1)
                wait(pe, yo_ready, c)
                for f in range(3):
                    l = mm(bank(6)[0:BC], wt("wf2", BC * f, BC * f + BC), gf[:, par, f, :],
                           start=(f == 0), stop=(f == 2))
                l.then_inc(wf2_made, 1)

            for f in range(3):
                l = mm(bank(7)[:, f:f + 1], wt("wf1", 128 * f, 128 * f + 128), col(T2), start=True, stop=True)
            l.then_inc(shift_made, 1)

            grapher_in(0, 0)
            grapher_out(0, 0)
            grapher_in(1, 1)
            mlp_in(0, 0)
            with pe.Fori(0, 3) as i:
                for u in range(2):
                    c = 2 * i + 1 + u
                    par = (1 + u) % 2
                    grapher_out(c, par)
                    mlp_out(c - 1, 1 - par)
                    grapher_in(c + 1, 1 - par)
                    mlp_in(c, par)
            grapher_out(7, 1)
            mlp_out(6, 0)
            mlp_in(7, 1)
            mlp_out(7, 1)

        @block.scalar
        def _(act):
            a = nc.scalar.activation

            act.wait_ge(pack_in, 16)
            a(col(R1), vec(V_V1), ACT.Sqrt, bias=vec(V_BNEPS))
            a(col(R2), vec(V_V2), ACT.Sqrt, bias=vec(V_BNEPS))
            a(col(RG), wt("vecs_g", 4, 5), ACT.Sqrt, bias=vec(V_BNEPS)).then_inc(roots_ready, 1)

            def square(k, m, par, centred, done):
                act.wait_ge(centred, m + 1)
                if k == 0:
                    wait(act, ssq_ready, m)
                a(sqr[:, k], (cen2 if k else cen)[:, par], ACT.Square).then_inc(done, 1)

            def take_xs(m, par):
                act.wait_ge(xs_turned, m + 1)
                wait(act, v1_made, m - 1)
                a(xs[0:BC, par, :], bank(7)[0:BC], ACT.Identity, bias=vec(V_N1B), scale=vec(V_N1G))\
                    .then_inc(xs_ready, 1)

            def take_qk(m, par):
                act.wait_ge(q_made, m + 1)
                wait(act, scores_made, WS * (m - 1))
                for b in range(B):
                    rows = slice(32 * b, 32 * b + 32)
                    l = a(stq[rows, par, b // 2, :, 64 * (b % 2):64 * (b % 2) + 64],
                          bank(6)[rows].rearrange("p (w t) -> p w t", t=WT), ACT.Copy,
                          scale=wt("scales", 3, 4)[rows])
                l.then_inc(stq_ready, 1)
                act.wait_ge(k_made, m + 1)
                for i in range(NH):
                    base = kmv[:, par, 0, i, :]
                    dst = bass.AP(base.tensor, base.offset, [
                        base.ap[0], [2 * NH * WT, WS // 2], [NH * WT + (NH - 1 - 2 * i) * WT, 2], [1, WT]])
                    l = a(dst, bank(7).rearrange("p (w e t) -> p w e t", e=2, t=WT), ACT.Copy,
                          scale=wt("scales", i, i + 1))
                l.then_inc(kmv_ready, 1)

            def take_v(m, par):
                wait(act, mixed, 4 * (m - 1))
                act.wait_ge(v0_made, m + 1)
                act.wait_ge(v1_made, m + 1)
                for k, halves in enumerate(PLACES):
                    for x, (odd, i) in enumerate(halves):
                        v = bank(6 + odd)[0:WT, 0:4 * BC].rearrange("k (x j c) -> k x j c", j=2, c=C)
                        dst = val[64 * x:64 * x + 64, par, :, :, k, 0:4 * HD]\
                            .rearrange("k t p (j c) -> k (t p) j c", j=2)[:, :, :, HD * x:HD * x + HD]
                        l = a(dst, v[:, :, :, HD * i:HD * i + HD], ACT.Copy)
                l.then_inc(val_ready, 1)

            def take_out(m):
                act.wait_ge(out_turned, m + 1)
                wait(act, projected, m)
                a(mt[0:BC, :], bank(6)[0:BC], ACT.Copy).then_inc(mt_ready, 1)

            def exps(t, pp):
                act.wait_ge(turned, t + 1)
                wait(act, mixed, t - 1)
                a(pt[:, pp, :], psum[:, 1024:1024 + 768], ACT.Exp).then_inc(probs_ready, 1)

            def attend(m, par, coming=True, after=True, before=True, second=True):
                for l in range(4):
                    if after or l < 3:
                        exps(4 * m + l + 1, (l + 1) % 2)
                    if l == 0 and after:
                        take_qk(m + 1, 1 - par)
                    if l == 1:
                        if coming:
                            square(0, m + 2, par, cen_ready, sqr_ready)
                        if after:
                            take_v(m + 1, 1 - par)
                    if l == 2 and before:
                        take_out(m - 1)
                    if l == 3:
                        if second:
                            square(1, m - 2, par, cen2_ready, sqr2_ready)
                        if coming:
                            take_xs(m + 2, par)

            square(0, 0, 0, cen_ready, sqr_ready)
            square(0, 1, 1, cen_ready, sqr_ready)
            take_xs(0, 0)
            take_xs(1, 1)
            act.wait_ge(zeroed, 2)
            take_qk(0, 0)
            take_v(0, 0)
            exps(0, 0)
            attend(0, 0, before=False, second=False)
            attend(1, 1, second=False)
            with act.Fori(1, 3) as i:
                attend(2 * i, 0)
                attend(2 * i + 1, 1)
            attend(6, 0, coming=False)
            attend(7, 1, coming=False, after=False)
            square(1, 6, 0, cen2_ready, sqr2_ready)
            take_out(7)
            square(1, 7, 1, cen2_ready, sqr2_ready)

            for u in range(B * NCH):
                act.wait_ge(conv_made, u + 1)
                wait(act, gated_ready, u - 3)
                a(gel[:, u % 4, :], bank(u % 4)[0:HID], ACT.Gelu).then_inc(gelu_ready, 1)

            act.wait_ge(folded, 1)
            for i in range(2):
                for u in range(4):
                    n = 4 * i + u
                    act.wait_ge(w1_made, n + 1)
                    a(chunk(h, n), bank(4 + u)[0:BC], ACT.Identity, bias=col(T1), scale=col(S1)).then_inc(h_ready, 1)

            def gelu_g(c, par):
                act.wait_ge(wg_made, c + 1)
                wait(act, w2_made, c - 1)
                for p in range(2):
                    a(gg[:, par, p, :], bank(p)[0:BC], ACT.Gelu, bias=col(TG), scale=col(SG)).then_inc(gg_ready, 1)

            def gelu_f(c, par):
                act.wait_ge(wf1_made, c + 1)
                wait(act, wf2_made, c - 1)
                for f in range(3):
                    l = a(gf[:, par, f, :], bank(3 + f), ACT.Gelu, bias=small[:, BF + f:BF + f + 1])
                l.then_inc(gf_ready, 1)

            gelu_g(0, 0)
            act.wait_ge(shift_ready, 1)
            def gelus(i):
                for u in range(2):
                    gelu_g(2 * i + u + 1, 1 - u)
                    gelu_f(2 * i + u, u)

            gelus(0)
            with act.Fori(1, 3) as i:
                gelus(i)
            gelu_g(7, 1)
            gelu_f(6, 0)
            gelu_f(7, 1)

        @block.vector
        def _(dve):
            v = nc.vector

            def centre(k, m, par):
                if k == 0:
                    src = (xtok[:, m, :] if isinstance(m, int) else xtok[:, bass.ds(m, 1), :].rearrange(
                        "p a n -> p (a n)")).rearrange("p (g c) -> p g c", c=C)
                    wait(dve, xhat_ready, m - 1)
                    wait(dve, cen_ready, m)
                    summed, done, dst = sum_ready, cen_ready, cen[:, par]
                else:
                    src = bank(7)[:, 0:TOK * BC].rearrange("p (g c) -> p g c", c=C)
                    dve.wait_ge(x1_turned, m + 1)
                    if isinstance(m, int) and m >= 5:
                        dve.wait_ge(y_ready, m - 1)
                    summed, done, dst = sum2_ready, cen2_ready, cen2[:, par]
                v.tensor_reduce(sums[:, k, :], src, AX.X, ALU.add).then_inc(summed, 1)
                dve.wait_ge(summed, m + 1)
                v.scalar_tensor_tensor(dst, sums[:, k, :].unsqueeze(2).to_broadcast([128, GR, C]), -1.0 / C, src,
                                       ALU.mult, ALU.add).then_inc(done, 1)

            def variance(k, m):
                squared_, summed, done = ((sqr_ready, ssq_ready, var_ready), (sqr2_ready, ssq2_ready, var2_ready))[k]
                dve.wait_ge(squared_, m + 1)
                v.tensor_reduce(squares[:, k, :], sqr[:, k], AX.X, ALU.add).then_inc(summed, 1)
                dve.wait_ge(summed, m + 1)
                v.tensor_scalar(var[:, k, :], squares[:, k, :], 1.0 / C, LN_EPS, ALU.mult, ALU.add).then_inc(done, 1)

            def normalise(k, m, par):
                deviation = rstd[:, k, :].unsqueeze(2).to_broadcast([128, GR, C])
                if k == 0:
                    dve.wait_ge(rstd_ready, m + 1)
                    wait(dve, xs_turned, m)
                    v.tensor_tensor(xhat[:, :, :].rearrange("p k (b c) -> p (k b) c", c=C), cen[:, par],
                                    deviation, ALU.mult).then_inc(xhat_ready, 1)
                else:
                    dve.wait_ge(rstd2_ready, m + 1)
                    dve.wait_ge(gained_ready, m + 1)
                    v.tensor_tensor(cen2[:, par], gained[:, :, :], deviation, ALU.mult).then_inc(norm2_ready, 1)

            dve.wait_ge(x_in, 16)
            for m in range(2):
                centre(0, m, m)
            variance(0, 0)
            normalise(0, 0, 0)
            variance(0, 1)
            normalise(0, 1, 1)
            dve.wait_ge(pack_in, 16)
            v.tensor_copy(posr[:, :], wt("posi"))
            for odd in range(2):
                for i in range(NH):
                    at = WT * (NH - 1 - i if odd else i)
                    for p in range(2):
                        l = v.tensor_copy(biasr[0:WT, odd, p, at:at + WT], wt("rpb", WT * i, WT * i + WT))
            l.then_inc(bias_high, 1)
            dve.wait_ge(bias_high, 1)
            for odd in range(2):
                for i in range(NH):
                    at = WT * (NH - 1 - i if odd else i)
                    for p in range(2):
                        l = v.tensor_tensor(biasr[64:128, odd, p, at:at + WT], wt("rpb", WT * i, WT * i + WT),
                                            biasr[0:WT, odd, p, at:at + WT].bitcast(F32), ALU.subtract)
            l.then_inc(bias_ready, 1)
            dve.wait_ge(roots_ready, 1)
            v.reciprocal(small[0:BC, R1:RG + 1], small[0:BC, R1:RG + 1]).then_inc(folding, 1)
            dve.wait_ge(folding, 1)
            norms = ((S1, R1, vec(V_G1), vec(V_B1), vec(V_M1), vec(V_BE1), T1),
                     (S2, R2, vec(V_G2), vec(V_B2), vec(V_M2), vec(V_BE2), T2),
                     (SG, RG, wt("vecs_g", 1, 2), wt("vecs_g", 0, 1), wt("vecs_g", 3, 4), wt("vecs_g", 2, 3), TG))
            for s, r, gain, b0, mean, beta, t in norms:
                v.tensor_tensor(col(s), col(r), gain, ALU.mult)
                l = v.tensor_tensor(col(t), b0, mean, ALU.subtract)
            l.then_inc(folding, 1)
            dve.wait_ge(folding, 2)
            for s, r, gain, b0, mean, beta, t in norms:
                l = v.scalar_tensor_tensor(col(t), col(t), col(s), beta, ALU.mult, ALU.add)
            v.tensor_tensor(wca[:, :], wt("pin"), wt("dwa"), ALU.mult)
            v.tensor_tensor(wcb[:, :], wt("pin")[0:C * TB], wt("dwb"), ALU.mult).then_inc(folded, 1)

            def subtract_max(m, w):
                n = WS * m + w
                dve.wait_ge(scores_made, n + 1)
                s = bank(w % 2, 2 * NH * WT).rearrange("p (g k) -> p g k", k=WT)
                v.tensor_reduce(mx[:, w % 2, :], s, AX.X, ALU.max).then_inc(max_ready, 1)
                dve.wait_ge(max_ready, n + 1)
                wait(dve, turned, 4 * m + w // 2 - 1)
                dst = diff[:, (w // 2) % 2, :, NH * WT * (w % 2):NH * WT * (w % 2 + 1)]
                v.tensor_tensor(dst.rearrange("p i (h k) -> p i h k", k=WT), s.rearrange("p (i h) k -> p i h k", i=2),
                                mx[:, w % 2, :].rearrange("p (i h) -> p i h", i=2).unsqueeze(3)
                                .to_broadcast([128, 2, NH, WT]), ALU.subtract).then_inc(diff_ready, 1)

            def divide(m, half):
                g = 2 * m + half
                dve.wait_ge(mixed, 2 * g + 2)
                o = bank(4 + half, 12 * VW).rearrange("p (n c) -> p n c", c=VW)
                v.reciprocal(rz[:, half], o[:, :, 4 * HD:4 * HD + 2]).then_inc(rz_ready, 1)
                dve.wait_ge(rz_ready, g + 1)
                wait(dve, out_turned, m)
                for j in range(2):
                    rows = slice(64 * j, 64 * j + 64)
                    l = v.tensor_tensor(ot[rows, half].rearrange("p n (x d) -> p n x d", d=HD),
                                        o[rows, :, 2 * HD * j:2 * HD * j + 2 * HD]
                                        .rearrange("p n (x d) -> p n x d", d=HD),
                                        rz[rows, half].unsqueeze(3).to_broadcast([64, 12, 2, HD]), ALU.mult)
                l.then_inc(ot_ready, 1)

            def residual(m, par):
                dve.wait_ge(projected, m + 1)
                if isinstance(m, int) and m >= 5:
                    dve.wait_ge(x1_ready, m - 1)
                src = bank(6)[0:BC].rearrange("p (w r s) -> p w r s", r=WS, s=WS)
                add = chunk(xin[0:BC], m).rearrange("p (w r s) -> p w r s", r=WS, s=WS)
                dst = x1s[:, par]
                cut = WS - SHIFT
                v.tensor_tensor(dst[:, :, SHIFT:W - cut].rearrange("p r (w s) -> p w r s", s=WS),
                                src[:, 0:WS - 1], add[:, 0:WS - 1], ALU.add)
                v.tensor_tensor(dst[:, :, W - cut:W], src[:, WS - 1, :, 0:cut], add[:, WS - 1, :, 0:cut], ALU.add)
                v.tensor_tensor(dst[:, :, 0:SHIFT], src[:, WS - 1, :, cut:], add[:, WS - 1, :, cut:], ALU.add)\
                    .then_inc(x1s_ready, 1)

            def copy_rows(m, par):
                wait(dve, v1_made, m - 1)
                v.tensor_copy(xs[BC:KX, par, :], chunk(xin[BC:KX], m)).then_inc(rows_ready, 1)

            def attend(m, par, coming=True, after=True, before=True, second=True):
                def ahead(l, e):
                    if after or l < 2:
                        if l < 2:
                            subtract_max(m, 2 * l + 4 + e)
                        else:
                            subtract_max(m + 1, 2 * l - 4 + e)

                if before:
                    divide(m - 1, 1)
                ahead(0, 0)
                ahead(0, 1)
                if coming:
                    centre(0, m + 2, par)
                ahead(1, 0)
                if coming:
                    variance(0, m + 2)
                ahead(1, 1)
                divide(m, 0)
                if coming:
                    normalise(0, m + 2, par)
                    copy_rows(m + 2, par)
                ahead(2, 0)
                ahead(2, 1)
                if second:
                    centre(1, m - 2, par)
                ahead(3, 0)
                if second:
                    variance(1, m - 2)
                ahead(3, 1)
                if second:
                    normalise(1, m - 2, par)
                if before:
                    residual(m - 1, 1 - par)

            dve.wait_ge(feat_in, 32)
            copy_rows(0, 0)
            copy_rows(1, 1)
            for w in range(4):
                subtract_max(0, w)
            attend(0, 0, before=False, second=False)
            attend(1, 1, second=False)
            with dve.Fori(1, 3) as i:
                attend(2 * i, 0)
                attend(2 * i + 1, 1)
            attend(6, 0, coming=False)
            attend(7, 1, coming=False, after=False)
            divide(7, 1)
            centre(1, 6, 0)
            variance(1, 6)
            normalise(1, 6, 0)
            residual(7, 1)
            centre(1, 7, 1)
            variance(1, 7)
            normalise(1, 7, 1)

            def edges(b):
                j = b % 2
                dve.wait_ge(stack_in[j], 16 * (TA + TB) * (b // 2 + 1))
                for n, (stack, rows) in enumerate(((sta, C * TA), (stb, C * TB))):
                    image = stack[:, j].rearrange("k (h w) -> k h w", w=W)
                    for side, w in enumerate((0, W - 1)):
                        l = v.tensor_scalar(image[:, :, w:w + 1], image[:, :, w:w + 1],
                                            wt("edge", 2 * n + side, 2 * n + side + 1)[0:rows], None, ALU.mult)
                l.then_inc(edged, 1)

            v.memset(gated[:], 0.0).then_inc(hpart_ready, 1)
            dve.wait_ge(hpart_ready, 1)
            edges(0)
            for b in range(B):
                for c in range(NCH):
                    u = NCH * b + c
                    if c == NCH // 2 and b + 1 < B:
                        edges(b + 1)
                    dve.wait_ge(gelu_ready, u + 1)
                    v.tensor_tensor(gated[64 * (b % 2):64 * (b % 2) + HID, b // 2, c * CH:(c + 1) * CH],
                                    bank(u % 4)[64:64 + HID], gel[:, u % 4, :], ALU.mult).then_inc(gated_ready, 1)

            def parity_minima(n):
                dve.wait_ge(h_ready, n + 1)
                here = chunk(h, n)
                part = hmin if n == 0 else hpart[:, n % 2]
                v.tensor_reduce(part[:, :, :], here.rearrange("p (r q w) -> p q w r", q=2, w=W), AX.X, ALU.min)\
                    .then_inc(hpart_ready, 1)
                v.tensor_reduce(wmin[:, 8 * n:8 * n + 8, :], here.rearrange("p (r x q) -> p r q x", q=2, x=W // 2),
                                AX.X, ALU.min)
                if n:
                    dve.wait_ge(hpart_ready, n + 2)
                    v.tensor_tensor(hmin[:, :, :], hmin[:, :, :], hpart[:, n % 2], ALU.min).then_inc(hmin_ready, 1)
                    dve.wait_ge(hmin_ready, n)

            for i in range(2):
                for u in range(4):
                    n = 4 * i + u
                    dve.wait_ge(pout_made, n + 1)
                    v.tensor_tensor(chunk(x2, n), bank(u)[0:BC],
                                    x1[:, 8 * n:8 * n + 8, :].rearrange("p r w -> p (r w)"), ALU.add)\
                        .then_inc(x2_ready, 1)
                for u in range(4):
                    parity_minima(4 * i + u)
            dve.wait_ge(shift_made, 1)
            v.tensor_tensor(small[:, BF:BF + 3], bank(7)[:, 0:3], wt("bf1"), ALU.add).then_inc(shift_ready, 1)

            def nearest(c, par):
                wait(dve, xj_ready, c - 1)
                for q in range(2):
                    wm = wmin[:, bass.ts(c, 8), :].rearrange("p (r q) x -> p q r x", q=2)[:, q]
                    v.tensor_tensor(near[:, par].rearrange("p (r q) (w x) -> p q r w x", q=2, x=2)[:, q],
                                    hmin[:, q, :].rearrange("p (w x) -> p w x", x=2).unsqueeze(1)
                                    .to_broadcast([BC, 4, W // 2, 2]),
                                    wm.unsqueeze(2).to_broadcast([BC, 4, W // 2, 2]), ALU.min)\
                        .then_inc(near_ready, 1)

            def add_shortcut(c, par):
                dve.wait_ge(w2_made, c + 1)
                wait(dve, wf1_made, c - 1)
                v.scalar_tensor_tensor(x3[:, par, :], bank(2)[0:BC], col(S2), chunk(x2, c), ALU.mult, ALU.add)\
                    .then_inc(x3_ready, 1)

            def finish(i, par):
                dve.wait_ge(wf2_made, 2 * i + par + 1)
                wait(dve, stored[par], 16 * i)
                v.tensor_scalar(yo[:, par, :], bank(6)[0:BC], vec(V_BF2), None, ALU.add).then_inc(yo_ready, 1)

            nearest(0, 0)
            nearest(1, 1)
            add_shortcut(0, 0)
            def two_chunks(i):
                for u in range(2):
                    c, par = 2 * i + 1 + u, 1 - u
                    add_shortcut(c, par)
                    nearest(c + 1, 1 - par)
                    finish(i, u)

            two_chunks(0)
            with dve.Fori(1, 3) as i:
                two_chunks(i)
            add_shortcut(7, 1)
            finish(3, 0)
            finish(3, 1)
    return nc


def lay_out(a):
    import numpy as np

    f = np.float32
    img, half = np.arange(B), np.arange(2)

    def blocks(w, rows=None, cols=None):
        o, n = w.shape
        m = np.zeros((B * n, B * o), f)
        for b in range(B):
            m[n * b:n * b + n, o * b:o * b + o] = w.T
        return m

    x = np.roll(a["x"], (-SHIFT, -SHIFT), axis=(2, 3))
    x = x.reshape(BC, H // WS, WS, W // WS, WS).transpose(0, 1, 3, 2, 4).reshape(BC, NT)

    last_row = np.arange(H) >= H - SHIFT
    last_col = np.arange(W) >= W - SHIFT
    region = (2 * last_row[:, None] + last_col[None, :]).reshape(H // WS, WS, W // WS, WS)
    region = region.transpose(0, 2, 1, 3).reshape(NT)
    feat = np.zeros((1 + NREG, NT), f)
    feat[0] = 1.0
    for r in range(NREG):
        feat[1 + r] = region == r

    qkv_w, qkv_b = a["L0_conv_qkv_w"], a["L0_conv_qkv_b"]
    p = {n: np.zeros(shape, f) for n, shape in PACK.items()}
    for b in range(B):
        rows = slice(C * b, C * b + C)
        p["wq"][rows, 32 * b:32 * b + C] = qkv_w[0:C].T
        p["wk"][rows, 32 * b:32 * b + C] = qkv_w[C:2 * C].T
        p["wv"][rows, rows] = qkv_w[2 * C:].T
        p["wq"][BC, 32 * b:32 * b + C] = qkv_b[0:C]
        p["wk"][BC, 32 * b:32 * b + C] = qkv_b[C:2 * C]
        p["wv"][BC, rows] = qkv_b[2 * C:]
        for r in range(NREG):
            p["wq"][BC + 1 + r, 32 * b + C + r] = 1.0
            p["wk"][BC, 32 * b + C + r] = MASKED
            p["wk"][BC + 1 + r, 32 * b + C + r] = -MASKED
            p["scales"][32 * b + C + r, :] = 1.0
        for i in range(NH):
            p["scales"][32 * b + HD * i:32 * b + HD * i + HD, i] = 1.0
        p["scales"][32 * b:32 * b + C, 3] = HD ** -0.5
        pair, j = divmod(b, 2)
        for y, (odd, i) in enumerate(place for halves in PLACES for place in halves):
            at, to = 2 * C * pair + HD * y, BC * (2 * odd + j) + C * b
            p["wproj"][at:at + HD, to:to + C] = a["L0_conv_proj_w"][:, HD * i:HD * i + HD].T
        for odd in range(2):
            p["wproj"][BC, 2 * BC * odd + C * b:2 * BC * odd + C * b + C] = a["L0_conv_proj_b"]
        p["pout"][64 * j:64 * j + HID, BC * pair + C * b:BC * pair + C * b + C] = a["L0_conv_pout_w"].T
        cols = slice(BC * pair + G2 * j, BC * pair + G2 * j + G2)
        p["wgh"][rows, cols] = a["L1_conv_wg"][:, 0:C].T
        p["wgx"][rows, cols] = a["L1_conv_wg"][:, C:].T
        p["w2"][G2 * j:G2 * j + G2, BC * pair + C * b:BC * pair + C * b + C] = a["L1_conv_w2"].T
        p["wf1"][rows, F4 * b:F4 * b + F4] = a["L1_conv_wf1"].T
    y, z = np.divmod(np.arange(WT), WS)
    at = (y[:, None] - y[None, :] + WS - 1) * (2 * WS - 1) + z[:, None] - z[None, :] + WS - 1
    p["rpb"][:] = a["L0_conv_rpb_table"][at].transpose(0, 2, 1).reshape(WT, NH * WT)
    p["posi"][:] = np.tile(np.eye(WT, dtype=f), (2, 2))
    p["eye"][:] = np.eye(128, dtype=f)
    per_channel = ["L0_conv_norm1_g", "L0_conv_norm1_b", "L1_conv_b1",
                   "L1_conv_g1", "L1_conv_be1", "L1_conv_m1", "L1_conv_v1", "L1_conv_b2", "L1_conv_g2",
                   "L1_conv_be2", "L1_conv_m2", "L1_conv_v2", "L1_conv_bf2"]
    for n, name in enumerate(per_channel):
        p["vecs"][:, n] = np.tile(a[name], B)
    p["gain2"][:], p["shift2"][:] = a["L0_conv_norm2_g"], a["L0_conv_norm2_b"]
    p["vecs"][:, V_BNEPS] = BN_EPS
    for n, name in enumerate(["bg", "gg", "beg", "mg", "vg"]):
        p["vecs_g"][:, n] = np.tile(a["L1_conv_" + name], 2)
    p["bf1"][:] = np.tile(a["L1_conv_bf1"], B).reshape(3, 128).T
    pin, taps = a["L0_conv_pin_w"], a["L0_conv_dw_w"].reshape(2 * HID, 9)
    for part in range(2):
        outs, src = slice(64 * part, 64 * part + HID), slice(HID * part, HID * part + HID)
        for t in range(TA + TB):
            name, k = ("dwa", t) if t < TA else ("dwb", t - TA)
            if t < TA:
                p["pin"][C * t:C * t + C, outs] = pin[src].T
            p[name][C * k:C * k + C, outs] = taps[None, src, t]
    p["w1"][:] = blocks(a["L1_conv_w1"])
    p["wf2"][:] = blocks(a["L1_conv_wf2"]).reshape(3, 128, BC).transpose(1, 0, 2).reshape(128, 3 * BC)
    for n, (first, count) in enumerate(((0, TA), (TA, TB))):
        for k in range(count):
            for side, reach in enumerate((0, 2)):
                p["edge"][C * k:C * k + C, 2 * n + side] = (first + k) % 3 != reach
    pack = np.zeros((128, PACK_W), f)
    for n, (r, c) in PACK.items():
        pack[0:r, PACK_AT[n]:PACK_AT[n] + c] = p[n]
    tokens = x.reshape(BC, NT // 128, 128).transpose(2, 1, 0).reshape(128, -1)
    return {"xw": np.ascontiguousarray(x), "xt": np.ascontiguousarray(tokens), "feat": feat, "pack": pack}


def kernel(**inputs):
    import numpy as np
    import concourse.bacc as bacc
    from concourse.bass_utils import run_bass_kernel_spmd

    arrays = lay_out({name: np.asarray(value) for name, value in inputs.items()})
    nc = bacc.Bacc("TRN2", target_bir_lowering=False, num_devices=1)
    args = [nc.dram_tensor(n, v.shape, F32, kind="ExternalInput").ap() for n, v in arrays.items()]
    out = nc.dram_tensor("out", (B, C, H, W), F32, kind="ExternalOutput").ap()
    build(nc, *args, out)
    return run_bass_kernel_spmd(nc, [arrays], core_ids=[0]).results[0]["out"]
```

```python
from contextlib import ExitStack

import concourse.bass as bass
from concourse import mybir

F32 = mybir.dt.float32
F32R = mybir.dt.float32r
ALU = mybir.AluOpType
ACT = mybir.ActivationFunctionType
AX = mybir.AxisListType

B, C, H, W = 4, 24, 64, 64
NT = H * W
WS, SHIFT = 8, 4
NH, HD = 3, 8
HID = 63
BC = B * C
G2 = 2 * C
F4 = 4 * C
CH = 512
NCH = NT // CH
WT = WS * WS
NREG = 4
KX = BC + 1 + NREG
TOK = CH // 128
GR = TOK * B
PLANES4, PLANES5 = (((m + 1) * WS - SHIFT) * W * C // NT for m in (4, 5))
STACKS = ((0, PLANES4), (PLANES4, C))
RA, RB = (9 * (c1 - c0) for c0, c1 in STACKS)
MASKED = -100.0
LN_EPS, BN_EPS = 1e-5, 1e-5

PACK = {
    "eye": (128, 128), "wq": (KX, 128), "wk": (KX, 128), "wv": (KX, BC), "scales": (128, 4),
    "vecs": (BC, 14), "vecs_g": (BC, 5),
    "rpb": (WT, NH * WT), "posi": (128, 128),
    "wproj": (BC + 1, 4 * BC), "gain2": (128, C), "shift2": (128, C), "edge": (RA, 8),
    "bf1": (128, 3), "pina": (RA, 128), "pinb": (RB, 128), "dwa": (RA, 128), "dwb": (RB, 128),
    "pout": (128, 2 * BC), "w1": (BC, BC), "wg": (BC, 2 * BC), "wgh": (BC, 2 * BC), "wgx": (BC, 2 * BC),
    "w2": (BC, 2 * BC), "wf1": (BC, B * F4), "wf2": (128, 3 * BC),
}
PACK_AT, _at = {}, 0
for _name, (_r, _c) in PACK.items():
    PACK_AT[_name] = _at
    _at += _c
PACK_W = _at
PACK_LOADS = (0, PACK_AT["rpb"], PACK_AT["wproj"], PACK_W)
(V_N1G, V_N1B, V_B1, V_G1, V_BE1, V_M1, V_V1, V_B2, V_G2, V_BE2, V_M2, V_V2, V_BF2, V_BNEPS) = range(14)
PAD = 128
PLACES = (((0, 0), (0, 1)), ((0, 2), (1, 2)), ((1, 1), (1, 0)))
VW = 2 * 2 * HD + 2


def build(nc, xw, xt, feat, pack, out):
    scratch = nc.dram_tensor("scratch", [B, PAD + C * NT + PAD], F32, kind="Internal").ap()

    with ExitStack() as ctx:
        def sb(stack, name, shape, dt=F32):
            return stack.enter_context(nc.sbuf_tensor(name, shape, dt))

        def sem(name):
            return ctx.enter_context(nc.semaphore(name))

        psum = ctx.enter_context(nc.psum_tensor("psum", [128, 8 * 512], F32))

        def bank(n, cols=512):
            return psum[:, 512 * n:512 * n + cols]

        pk = sb(ctx, "pk", [128, PACK_W])
        small = sb(ctx, "small", [128, 16])
        wca = sb(ctx, "wca", [RA, 128])
        wcb = sb(ctx, "wcb", [RB, 128])
        sta = sb(ctx, "sta", [RA, 2, NT])
        stb = sb(ctx, "stb", [RB, 2, NT])

        def wt(name, c0=0, c1=None):
            r, c = PACK[name]
            a = PACK_AT[name]
            return pk[0:r, a + c0:a + (c if c1 is None else c1)]

        def vec(n):
            return wt("vecs", n, n + 1)

        stacked = [sta[0:BC, 0, :], stb[0:BC, 0, :]]

        until_x2 = ExitStack()
        x1 = sb(until_x2, "x1", [BC, H, W])

        att = ExitStack()
        xin = sb(att, "xin", [KX, NT])
        xtok = sb(att, "xtok", [128, NCH, GR * C])
        biasr = sb(att, "biasr", [128, 2, 2, NH * WT], F32R)
        posr = sb(att, "posr", [128, 128], F32R)
        cen = sb(att, "cen", [128, 2, GR, C])
        cen2 = sb(att, "cen2", [128, 2, GR, C])
        sqr = sb(att, "sqr", [128, 2, GR, C])
        sums = sb(att, "sums", [128, 2, GR])
        squares = sb(att, "squares", [128, 2, GR])
        var = sb(att, "var", [128, 2, GR])
        rstd = sb(att, "rstd", [128, 2, GR])
        power = sb(att, "power", [128, GR])
        xhat = sb(att, "xhat", [128, TOK, BC])
        gained = sb(att, "gained", [128, GR, C])
        ytok = sb(att, "ytok", [128, 2, B, TOK * C])
        xs = sb(att, "xs", [KX, 2, CH])
        stq = sb(att, "stq", [128, 2, 2, WS, 128])
        kmv = sb(att, "kmv", [128, 2, WS, NH, WT])
        val = sb(att, "val", [128, 2, WS // 2, 2, 3, VW])
        diff = sb(att, "diff", [128, 2, 2, 2 * NH * WT])
        mx = sb(att, "mx", [128, 2, 2 * NH])
        pt = sb(att, "pt", [128, 2, 768])
        rz = sb(att, "rz", [128, 2, 12, 2])
        ot = sb(att, "ot", [128, 2, 2, 12, 16])
        mt = sb(att, "mt", [BC + 1, CH])
        x1s = sb(att, "x1s", [BC, 2, 8, W])
        att.close()

        late = ExitStack()
        gated = sb(late, "gated", [128, 2, NT])
        gel = sb(late, "gel", [64, 4, CH])
        x2 = sb(late, "x2", [BC, NT])
        hmin = sb(late, "hmin", [BC, 2, W])
        hpart = sb(late, "hpart", [BC, 2, 2, W])
        wmin = sb(late, "wmin", [BC, H, 2])
        near = sb(late, "near", [BC, 2, 8, W])
        xj = sb(late, "xj", [BC, 2, CH])
        gg = sb(late, "gg", [BC, 2, 2, CH])
        x3 = sb(late, "x3", [BC, 2, CH])
        x3r = sb(late, "x3r", [BC, 2, 2, CH], F32R)
        gf = sb(late, "gf", [128, 2, 3, CH])
        yo = sb(late, "yo", [BC, 2, CH])
        wf1r = sb(late, "wf1r", [BC, 2, B * F4], F32R)
        wf2r = sb(late, "wf2r", [128, 2, 3 * BC], F32R)
        late.close()
        until_x2.close()
        hidden = ExitStack()
        gfr = sb(hidden, "gfr", [128, 2, 3, 2, CH], F32R)
        hidden.close()

        first_x_in, x_in, channels_in, rows_in = (sem(n) for n in ("first_x_in", "x_in", "channels_in", "rows_in"))
        first_in, bias_in, weights_in = sem("first_in"), sem("bias_in"), sem("weights_in")
        zeroed = sem("zeroed")
        bias_high, bias_ready = sem("bias_high"), sem("bias_ready")
        roots_ready, folding, folded = sem("roots_ready"), sem("folding"), sem("folded")
        shift_made, shift_ready = sem("shift_made"), sem("shift_ready")
        sum_ready, cen_ready, sqr_ready, ssq_ready, var_ready, rstd_ready, xhat_ready, xs_turned, xs_ready = (
            sem(n) for n in ("sum_ready", "cen_ready", "sqr_ready", "ssq_ready", "var_ready", "rstd_ready",
                             "xhat_ready", "xs_turned", "xs_ready"))
        rows_ready = sem("rows_ready")
        x1_turned, sum2_ready, cen2_ready, sqr2_ready, ssq2_ready, var2_ready, rstd2_ready = (
            sem(n) for n in ("x1_turned", "sum2_ready", "cen2_ready", "sqr2_ready", "ssq2_ready", "var2_ready",
                             "rstd2_ready"))
        root_ready = sem("root_ready")
        root2_ready, last_y = sem("root2_ready"), sem("last_y")
        gained_ready, norm2_ready, y_ready = sem("gained_ready"), sem("norm2_ready"), sem("y_ready")
        wrap_stored = sem("wrap_stored")
        y_stored = [sem(f"y_stored{par}") for par in range(2)]
        q_made, k_made, stq_ready, kmv_ready = (sem(n) for n in ("q_made", "k_made", "stq_ready", "kmv_ready"))
        v0_made, v1_made, val_ready = sem("v0_made"), sem("v1_made"), sem("val_ready")
        scores_made, max_ready, diff_ready, turned, probs_ready, mixed = (
            sem(n) for n in ("scores_made", "max_ready", "diff_ready", "turned", "probs_ready", "mixed"))
        rz_ready, ot_ready, out_turned, mt_ready, projected, x1s_ready, x1_ready = (
            sem(n) for n in ("rz_ready", "ot_ready", "out_turned", "mt_ready", "projected", "x1s_ready", "x1_ready"))
        bordered, edged = ([sem(f"{name}{n}") for n in range(2)] for name in ("bordered", "edged"))
        pads_in, stack_in = sem("pads_in"), [[sem(f"stack_in{n}{j}") for j in range(2)] for n in range(2)]
        conv_made, gelu_ready, gated_ready = sem("conv_made"), sem("gelu_ready"), sem("gated_ready")
        pout_made, x2_ready, w1_made, h_ready = sem("pout_made"), sem("x2_ready"), sem("w1_made"), sem("h_ready")
        h_doubled = sem("h_doubled")
        gg_ready, gf_full, gf_high = sem("gg_ready"), sem("gf_full"), sem("gf_high")
        weights_high, x3_sum, x3_high = sem("weights_high"), sem("x3_sum"), sem("x3_high")
        hpart_ready, hmin_ready = sem("hpart_ready"), sem("hmin_ready")
        near_ready, xj_ready, wg_made = sem("near_ready"), sem("xj_ready"), sem("wg_made")
        gf_low = [sem(f"gf_low{p}") for p in range(2)]
        w2_made, x3_ready, wf1_made, wf2_made, yo_ready = (
            sem(n) for n in ("w2_made", "x3_ready", "wf1_made", "wf2_made", "yo_ready"))
        xj_in = [sem(f"xj_in{par}") for par in range(2)]
        stored = [sem(f"stored{par}") for par in range(2)]

        S1, T1, S2, T2, SG, TG, BF = 0, 1, 2, 3, 4, 5, 6
        R1, R2, RG, ROOT = 9, 10, 11, 12

        def col(n, rows=BC):
            return small[0:rows, n:n + 1]

        def wait(eng, s, count):
            if isinstance(count, int) and count <= 0:
                return
            eng.wait_ge(s, count)

        def chunk(buf, n):
            return buf[:, bass.ts(n, CH)]

        def keys_of(i, par):
            base = kmv[:, par, 0, i, :]
            dst = bass.AP(base.tensor, base.offset, [
                base.ap[0], [2 * NH * WT, WS // 2], [NH * WT + (NH - 1 - 2 * i) * WT, 2], [1, WT]])
            return dst, bank(7).rearrange("p (w e t) -> p w e t", e=2, t=WT)

        def gain_of(m):
            if isinstance(m, int) and m == NCH - 1:
                return xhat[:, :, :].rearrange("p k (b c) -> p (k b) c", c=C)
            return gained[:, :, :]

        def shift_of(par):
            shift = wt("shift2").unsqueeze(1).unsqueeze(1).to_broadcast([128, TOK, B, C])
            return (ytok[:, par].rearrange("p b (k c) -> p k b c", c=C),
                    cen2[:, par].rearrange("p (k b) c -> p k b c", b=B), shift)

        def conv_bank(u):
            return bank(u if u < NCH else u % 4)

        def y_count(m):
            return 16 * (m // 2 + 2)

        def load_copies(queue, b, n, c0, c1, window_rows=range(3)):
            first, last = STACKS[n]
            for y in window_rows:
                src = scratch[b]
                off = PAD + (y - 1) * W - 1 + c0 * NT
                src = bass.AP(src.tensor, src.offset + off, [[NT, c1 - c0], [1, 3], [1, NT]])
                at = 3 * ((last - first) * y + c0 - first)
                queue.dma_start((sta, stb)[n][at:at + 3 * (c1 - c0), b % 2, :], src).then_inc(stack_in[n][b % 2], 16)

        def stack_count(b, n):
            return 16 * 3 * (b // 2 + 1 + (n == 1 and b % 2 == 0))

        block = ctx.enter_context(nc.Block())

        @block.sync
        def _(sp):
            tokens = xtok[:, :, :].rearrange("p m n -> p (m n)")
            two = 2 * GR * C
            p0, p1, p2, p3 = PACK_LOADS
            sp.dma_start(tokens[:, 0:two], xt[:, 0:two]).then_inc(first_x_in, 16)
            sp.dma_start(pk[:, p0:p1], pack[:, p0:p1]).then_inc(first_in, 16)
            sp.dma_start(xin[BC:KX, :], feat).then_inc(rows_in, 16)
            sp.dma_start(pk[:, p1:p2], pack[:, p1:p2]).then_inc(bias_in, 16)
            sp.dma_start(tokens[:, two:], xt[:, two:]).then_inc(x_in, 16)
            sp.dma_start(pk[:, p2:p3], pack[:, p2:p3]).then_inc(weights_in, 16)
            sp.dma_start(xin[0:BC, :], xw).then_inc(channels_in, 16)
            sp.dma_start(bass.AP(scratch.tensor, 0, [[2 * PAD + C * NT, B], [PAD + C * NT, 2], [1, PAD]]),
                         feat[0:1, 0:2 * B * PAD].rearrange("o (b e n) -> (o b) e n", b=B, e=2))\
                .then_inc(pads_in, 16)

            def store_y(m, par):
                if isinstance(m, int) and m == NCH - 1:
                    sp.wait_ge(last_y, 1)
                else:
                    sp.wait_ge(y_ready, m + 1)
                at = (8 * m - SHIFT) * W
                parts = [(slice(0, 128), at, y_stored[par])]
                if isinstance(m, int) and m == 0:
                    parts = [(slice(0, 64), NT + at, wrap_stored), (slice(64, 128), 0, y_stored[par])]
                for own, token, done in parts:
                    if done is not wrap_stored and len(parts) > 1:
                        sp.wait_ge(wrap_stored, 16)
                    count = TOK * (own.stop - own.start)
                    dst = scratch[:, PAD:PAD + C * NT].rearrange("b (t c) -> b t c", c=C)[:, bass.ds(token, count), :]
                    sp.dma_start(dst.rearrange("b (p k) c -> p b (k c)", k=TOK), ytok[own, par])\
                        .then_inc(done, 16)

            store_y(0, 0)
            store_y(1, 1)
            with sp.Fori(1, 3) as i:
                store_y(2 * i, 0)
                store_y(2 * i + 1, 1)
            sp.wait_ge(pads_in, 16)
            for m in (4, 5):
                sp.wait_ge(y_stored[m % 2], y_count(m))
            load_copies(sp, 0, 1, PLANES4, PLANES5)
            store_y(6, 0)
            store_y(7, 1)
            for m in (6, 7):
                sp.wait_ge(y_stored[m % 2], y_count(m))
            load_copies(sp, 0, 1, PLANES5, C, (0, 1))
            for b in range(1, B):
                if b >= 2:
                    sp.wait_ge(conv_made, NCH * (b - 1))
                if b >= 2:
                    load_copies(sp, b, 0, 0, PLANES4)
                load_copies(sp, b, 1, PLANES4, C)
            out_rows = out.rearrange("b c h w -> (b c) (h w)")

            def place_xj(c):
                sp.wait_ge(xj_ready, c + 1)
                for p in range(2):
                    own, other = slice(G2 * p, G2 * p + G2), slice(G2 * (1 - p), G2 * (1 - p) + G2)
                    sp.dma_start(chunk(stacked[p], c)[other], xj[own, c % 2, :]).then_inc(xj_in[c % 2], 16)

            for c in (1, 2, 3):
                place_xj(c)
            for c in range(NCH):
                if c + 4 < NCH:
                    place_xj(c + 4)
                sp.wait_ge(yo_ready, c + 1)
                sp.dma_start(out_rows[:, c * CH:(c + 1) * CH], yo[:, c % 2, :]).then_inc(stored[c % 2], 16)
            for par in range(2):
                sp.wait_ge(stored[par], 16 * (NCH // 2 + 1))

        @block.gpsimd
        def _(pool):
            g = nc.gpsimd
            for par in range(2):
                g.memset(stq[:, par], 0.0).then_inc(stored[par], 16)
            g.memset(power[:], -0.5).then_inc(y_stored[0], 16)
            g.memset(mt[:], 1.0).then_inc(y_stored[1], 16)
            g.memset(val[:], 0.0).then_inc(zeroed, 1)
            pool.wait_ge(zeroed, 1)
            blocks = val[:, :, :, :, :, :].rearrange("k a t p n c -> k (a t p n) c")
            for x in range(2):
                l = g.memset(blocks[64 * x:64 * x + 64, :, 2 * 2 * HD + x:2 * 2 * HD + x + 1], 1.0)
            l.then_inc(zeroed, 1)

            def root(k, n, varied, done):
                pool.wait_ge(varied, n)
                g.tensor_tensor(rstd[:, k, :], var[:, k, :], power[:, :], ALU.pow).then_inc(done, 1)

            def second_norm(i, par):
                m = 2 * i + par
                pool.wait_ge(cen2_ready, m + 1)
                g.tensor_tensor(gained[:, :, :], cen2[:, par],
                                wt("gain2").unsqueeze(1).to_broadcast([128, GR, C]), ALU.mult)\
                    .then_inc(gained_ready, 1)
                if not (isinstance(m, int) and m >= 6):
                    root(1, m + 1, var2_ready, rstd2_ready)
                pool.wait_ge(norm2_ready, m + 1)
                pool.wait_ge(y_stored[par], 16 * (i + 1))
                g.tensor_tensor(*shift_of(par), ALU.add).then_inc(y_ready, 1)

            def keep_x1(m, par):
                pool.wait_ge(x1s_ready, m + 1)
                r0 = 8 * m - SHIFT
                if isinstance(m, int) and m == 0:
                    g.tensor_copy(x1[:, H - SHIFT:H, :], x1s[:, par, 0:SHIFT])
                    g.tensor_copy(x1[:, 0:8 - SHIFT, :], x1s[:, par, SHIFT:8]).then_inc(x1_ready, 1)
                else:
                    g.tensor_copy(x1[:, bass.ds(r0, 8), :], x1s[:, par]).then_inc(x1_ready, 1)

            pool.wait_ge(weights_in, 16)

            def step(i, par, first=True, before=True, second=True):
                m = 2 * i + par
                if first:
                    root(0, m + 3, var_ready, rstd_ready)
                if second:
                    second_norm(i - 1, par)
                if before:
                    keep_x1(m - 1, 1 - par)

            step(0, 0, before=False, second=False)
            step(0, 1, second=False)
            with pool.Fori(1, 3) as i:
                step(i, 0)
                step(i, 1)
            step(3, 0, first=False)
            step(3, 1, first=False)
            second_norm(3, 0)
            keep_x1(7, 1)

            def low_f(c, par):
                pool.wait_ge(gf_high, 3 * c + 3)
                g.tensor_tensor(gfr[:, par, 2, 1, :], gf[:, par, 2, :], gfr[:, par, 2, 0, :].bitcast(F32),
                                ALU.subtract).then_inc(gf_low[1], 1)

            low_f(0, 0)
            low_f(1, 1)
            with pool.Fori(1, 4) as i:
                low_f(2 * i, 0)
                low_f(2 * i + 1, 1)

        @block.tensor
        def _(pe):
            mm = nc.tensor.matmul

            def make_qk(m, par):
                pe.wait_ge(xs_ready, m + 1)
                wait(pe, rows_ready, m + 1)
                wait(pe, x1s_ready, m - 2)
                mm(bank(6), wt("wq"), xs[:, par, :], start=True, stop=True).then_inc(q_made, 1)
                mm(bank(7), wt("wk"), xs[:, par, :], start=True, stop=True).then_inc(k_made, 1)

            def make_v(m, par):
                for odd, (free, made) in enumerate(((stq_ready, v0_made), (kmv_ready, v1_made))):
                    pe.wait_ge(free, m + 1)
                    for w in range(WS // 2):
                        t0 = (2 * w + odd) * WT
                        l = mm(bank(6 + odd)[0:WT, BC * w:BC * w + BC], xs[:, par, t0:t0 + WT], wt("wv"),
                               start=True, stop=True)
                    l.then_inc(made, 1)

            def turn_xhat(m):
                pe.wait_ge(xhat_ready, m + 1)
                for k in range(TOK):
                    l = nc.tensor.transpose(bank(7)[0:BC, 128 * k:128 * k + 128], xhat[:, k, :], wt("eye"))
                l.then_inc(xs_turned, 1)

            def turn_x1(m, par):
                pe.wait_ge(x1s_ready, m + 1)
                rows = x1s[:, par].rearrange("b r w -> b (r w)").rearrange("b (p k) -> b k p", k=TOK)
                for k in range(TOK):
                    l = nc.tensor.transpose(bank(7)[:, BC * k:BC * k + BC], rows[:, k, :],
                                            wt("eye", 0, BC)[0:BC])
                l.then_inc(x1_turned, 1)

            def scores(m, w, par):
                n = WS * m + w
                if w == 0:
                    pe.wait_ge(stq_ready, m + 1)
                    pe.wait_ge(kmv_ready, m + 1)
                wait(pe, diff_ready, n - 1)
                s = bank(w % 2, 2 * NH * WT)
                mm(s, posr[:, :], biasr[:, w % 2].rearrange("k p n -> k (p n)"), start=True, stop=True)
                for p in range(2):
                    l = mm(s[:, NH * WT * p:NH * WT * (p + 1)], stq[:, par, p, w, :],
                           kmv[:, par, w, :, :].rearrange("k h n -> k (h n)"), start=False, stop=True,
                           skip_group_check=True)
                l.then_inc(scores_made, 1)

            def turn(t, w0):
                pe.wait_ge(diff_ready, 2 * (t + 1))
                wait(pe, probs_ready, t)
                for p in range(2):
                    for k in range(3):
                        at = 384 * p + 128 * k
                        l = nc.tensor.transpose(psum[:, 1024 + at:1024 + at + 128],
                                                diff[:, (w0 // 2) % 2, p, 128 * k:128 * k + 128], wt("eye"))
                l.then_inc(turned, 1)

            def mix(m, l, par):
                t = 4 * m + l
                if l == 0:
                    pe.wait_ge(val_ready, m + 1)
                if l % 2 == 0:
                    wait(pe, ot_ready, 2 * m + l // 2 - 1)
                pe.wait_ge(probs_ready, t + 1)
                o = bank(4 + l // 2)
                for p in range(2):
                    for k in range(3):
                        at, src = VW * (6 * (l % 2) + 3 * p + k), 384 * p + 128 * k
                        x = mm(o[:, at:at + VW], pt[:, l % 2, src:src + 128], val[:, par, l, p, k, :],
                               start=True, stop=True)
                x.then_inc(mixed, 1)

            def turn_out(m, par):
                pe.wait_ge(ot_ready, 2 * m + 2)
                flat = ot[:, par].rearrange("k a n c -> k (a n c)")
                for k in range(4):
                    l = nc.tensor.transpose(bank(6)[0:BC, 128 * k:128 * k + 128], flat[:, BC * k:BC * k + BC],
                                            wt("eye"))
                l.then_inc(out_turned, 1)

            def project(m):
                pe.wait_ge(mt_ready, m + 1)
                src = mt[:, :].rearrange("k (t j q) -> k j t q", j=2, q=WT)
                dst = bank(6)[0:BC].rearrange("k (t e q) -> k e t q", e=2, q=WT)
                for e in range(2):
                    for j in range(2):
                        at = BC * (2 * e + j)
                        l = mm(dst[:, e], wt("wproj", at, at + BC), src[:, j], start=(j == 0), stop=(j == 1))
                l.then_inc(projected, 1)

            def attend(m, par, coming=True, after=True, before=True, second=True):
                for l in range(4):
                    t = 4 * m + l
                    if after or l < 3:
                        turn(t + 1, (2 * l + 2) % WS)
                    if after or l < 2:
                        for e in range(2):
                            if l < 2:
                                scores(m, 2 * l + 4 + e, par)
                            else:
                                scores(m + 1, 2 * l - 4 + e, 1 - par)
                    if l == 0 and after:
                        make_qk(m + 1, 1 - par)
                    if l == 1 and after:
                        make_v(m + 1, 1 - par)
                    if l == 2:
                        pe.wait_ge(val_ready, m + 2 if after else m + 1)
                        if before:
                            turn_out(m - 1, 1 - par)
                        if second:
                            turn_x1(m - 2, par)
                    if l == 3:
                        if before:
                            project(m - 1)
                        if coming:
                            if second:
                                pe.wait_ge(cen2_ready, m - 1)
                            turn_xhat(m + 2)
                    mix(m, l, par)

            pe.wait_ge(first_in, 16)
            turn_xhat(0)
            pe.wait_ge(zeroed, 2)
            make_qk(0, 0)
            make_v(0, 0)
            pe.wait_ge(bias_ready, 1)
            scores(0, 0, 0)
            scores(0, 1, 0)
            pe.wait_ge(val_ready, 1)
            turn_xhat(1)
            turn(0, 0)
            scores(0, 2, 0)
            scores(0, 3, 0)
            pe.wait_ge(weights_in, 16)
            attend(0, 0, before=False, second=False)
            attend(1, 1, second=False)
            with pe.Fori(1, 3) as i:
                attend(2 * i, 0)
                attend(2 * i + 1, 1)
            attend(6, 0, coming=False)
            attend(7, 1, coming=False, after=False)
            pe.wait_ge(cen2_ready, 6)
            pe.wait_ge(x1s_ready, 7)
            turn_x1(6, 0)
            turn_out(7, 1)
            project(7)
            pe.wait_ge(cen2_ready, 7)
            turn_x1(7, 1)

            pe.wait_ge(folded, 1)
            pe.wait_ge(cen2_ready, 8)
            def gated_out(n):
                pe.wait_ge(gated_ready, (B - 1) * NCH + n + 1)
                wait(pe, x2_ready, n - 1)
                for p in range(2):
                    l = mm(bank(4 + n % 2)[0:BC], wt("pout", BC * p, BC * p + BC), chunk(gated[:, p, :], n),
                           start=(p == 0), stop=(p == 1))
                l.then_inc(pout_made, 1)

            def first_product(n):
                pe.wait_ge(x2_ready, n + 1)
                wait(pe, h_doubled, n - 1)
                mm(bank(6 + n % 2)[0:BC], wt("w1"), chunk(x2, n), start=True, stop=True).then_inc(w1_made, 1)

            pe.wait_ge(edged[0], 1)
            for c in range(NCH):
                mm(conv_bank(c), wca[:, :], chunk(sta[:, 0], c), start=True, stop=False)
            for b in range(B):
                if b:
                    pe.wait_ge(edged[0], b + 1)
                pe.wait_ge(edged[1], b + 1)
                for c in range(NCH):
                    u = NCH * b + c
                    if b:
                        wait(pe, gated_ready, u - 3)
                        mm(conv_bank(u), wca[:, :], chunk(sta[:, b % 2], c), start=True, stop=False)
                    mm(conv_bank(u), wcb[:, :], chunk(stb[:, b % 2], c), start=False, stop=True)\
                        .then_inc(conv_made, 1)
                    if b == B - 1 and c >= 1:
                        gated_out(c - 1)
                    if b == B - 1 and c >= 2:
                        first_product(c - 2)
            gated_out(NCH - 1)
            first_product(NCH - 2)
            first_product(NCH - 1)

            def grapher_in_first():
                for p in range(2):
                    mm(bank(p)[0:BC], wt("wgh", BC * p, BC * p + BC), chunk(stacked[0], 0), start=True, stop=False)
                pe.wait_ge(xj_ready, 1)
                for p in range(2):
                    mm(bank(p)[0:BC], wt("wgx", BC * p, BC * p + BC), xj[:, 0, :], start=False, stop=True)\
                        .then_inc(wg_made, 1)

            def grapher_in(i, par):
                pe.wait_ge(xj_in[par], 32 * (i + par))
                wait(pe, gg_ready, 2 * (2 * i + par))
                for p in range(2):
                    mm(bank(p)[0:BC], wt("wg", BC * p, BC * p + BC), chunk(stacked[p], 2 * i + par),
                       start=True, stop=True).then_inc(wg_made, 1)

            PARTS = ((0, 0), (1, 0), (0, 1))

            def grapher_out(c, par):
                wait(pe, x3_ready, c)
                for p in range(2):
                    pe.wait_ge(gg_ready, 2 * c + p + 1)
                    l = mm(bank(2)[0:BC], wt("w2", BC * p, BC * p + BC), gg[:, par, p, :],
                           start=(p == 0), stop=(p == 1))
                l.then_inc(w2_made, 1)

            def mlp_in(c, par):
                pe.wait_ge(x3_ready, c + 1)
                wait(pe, gf_full, 3 * c)
                for f in range(3):
                    for n, (part, x_part) in enumerate(PARTS):
                        l = mm(bank(3 + f), wf1r[:, part, 128 * f:128 * f + 128], x3r[:, par, x_part, :],
                               start=(n == 0), stop=(n == 2))
                    l.then_inc(wf1_made, 1)

            def mlp_out(c, par):
                wait(pe, yo_ready, c)
                for f in range(3):
                    if f < 2:
                        pe.wait_ge(gf_low[0], 2 * c + f + 1)
                    else:
                        pe.wait_ge(gf_low[1], c + 1)
                    for n, (part, g_part) in enumerate(PARTS):
                        l = mm(bank(6)[0:BC], wf2r[:, part, BC * f:BC * f + BC], gfr[:, par, f, g_part, :],
                               start=(f == 0 and n == 0), stop=(f == 2 and n == 2))
                l.then_inc(wf2_made, 1)

            for f in range(3):
                l = mm(bank(3)[:, f:f + 1], wt("wf1", 128 * f, 128 * f + 128), col(T2), start=True, stop=True)
            l.then_inc(shift_made, 1)

            grapher_in_first()
            pe.wait_ge(h_doubled, NCH)
            grapher_out(0, 0)
            grapher_in(0, 1)
            mlp_in(0, 0)
            def chunk_step(i, u, before=True):
                c, par = 2 * i + 1 + u, 1 - u
                grapher_out(c, par)
                grapher_in(i + 1, u)
                if before:
                    mlp_out(c - 2, par)
                mlp_in(c, par)

            chunk_step(0, 0, before=False)
            chunk_step(0, 1)
            with pe.Fori(1, 3) as i:
                chunk_step(i, 0)
                chunk_step(i, 1)
            grapher_out(7, 1)
            mlp_out(5, 1)
            mlp_in(7, 1)
            mlp_out(6, 0)
            mlp_out(7, 1)

        @block.scalar
        def _(act):
            a = nc.scalar.activation

            def square(k, m, par, centred, done):
                act.wait_ge(centred, m + 1)
                if k == 0:
                    wait(act, ssq_ready, m)
                a(sqr[:, k], (cen2 if k else cen)[:, par], ACT.Square).then_inc(done, 1)

            def take_xs(m, par):
                act.wait_ge(xs_turned, m + 1)
                wait(act, v1_made, m - 1)
                a(xs[0:BC, par, :], bank(7)[0:BC], ACT.Identity, bias=vec(V_N1B), scale=vec(V_N1G))\
                    .then_inc(xs_ready, 1)

            def take_qk(m, par):
                act.wait_ge(q_made, m + 1)
                wait(act, scores_made, WS * (m - 1))
                for b in range(B):
                    rows = slice(32 * b, 32 * b + 32)
                    l = a(stq[rows, par, b // 2, :, 64 * (b % 2):64 * (b % 2) + 64],
                          bank(6)[rows].rearrange("p (w t) -> p w t", t=WT), ACT.Copy,
                          scale=wt("scales", 3, 4)[rows])
                l.then_inc(stq_ready, 1)
                if isinstance(m, int) and m == 0:
                    return
                act.wait_ge(k_made, m + 1)
                for i in range(NH):
                    dst, src = keys_of(i, par)
                    l = a(dst, src, ACT.Copy, scale=wt("scales", i, i + 1))
                l.then_inc(kmv_ready, 1)

            def take_v(m, par):
                wait(act, mixed, 4 * (m - 1))
                act.wait_ge(v0_made, m + 1)
                act.wait_ge(v1_made, m + 1)
                for k, halves in enumerate(PLACES):
                    for x, (odd, i) in enumerate(halves):
                        v = bank(6 + odd)[0:WT, 0:4 * BC].rearrange("k (x j c) -> k x j c", j=2, c=C)
                        dst = val[64 * x:64 * x + 64, par, :, :, k, 0:4 * HD]\
                            .rearrange("k t p (j c) -> k (t p) j c", j=2)[:, :, :, HD * x:HD * x + HD]
                        l = a(dst, v[:, :, :, HD * i:HD * i + HD], ACT.Copy)
                l.then_inc(val_ready, 1)

            def take_out(m):
                act.wait_ge(out_turned, m + 1)
                wait(act, projected, m)
                a(mt[0:BC, :], bank(6)[0:BC], ACT.Copy).then_inc(mt_ready, 1)

            def exps(t, pp):
                act.wait_ge(turned, t + 1)
                wait(act, mixed, t - 1)
                a(pt[:, pp, :], psum[:, 1024:1024 + 768], ACT.Exp).then_inc(probs_ready, 1)

            def attend(m, par, coming=True, after=True, before=True, second=True):
                for l in range(4):
                    if after or l < 3:
                        exps(4 * m + l + 1, (l + 1) % 2)
                    if l == 0 and after:
                        take_qk(m + 1, 1 - par)
                    if l == 1:
                        if coming:
                            square(0, m + 2, par, cen_ready, sqr_ready)
                        if after:
                            take_v(m + 1, 1 - par)
                    if l == 2 and before:
                        take_out(m - 1)
                    if l == 3:
                        if second:
                            square(1, m - 2, par, cen2_ready, sqr2_ready)
                        if coming:
                            take_xs(m + 2, par)
                    if l >= 2 and not after:
                        if l == 2:
                            act.wait_ge(pads_in, 16)
                            for n in (3, 4):
                                act.wait_ge(y_stored[n % 2], y_count(n))
                        load_copies(act, l - 2, 0, 0, PLANES4)

            for m in range(2):
                square(0, m, m, cen_ready, sqr_ready)
                act.wait_ge(var_ready, m + 1)
                wait(act, xhat_ready, m)
                a(rstd[:, 0, :], var[:, 0, :], ACT.Sqrt).then_inc(root_ready, 1)
            act.wait_ge(first_in, 16)
            a(col(R1), vec(V_V1), ACT.Sqrt, bias=vec(V_BNEPS))
            a(col(R2), vec(V_V2), ACT.Sqrt, bias=vec(V_BNEPS))
            a(col(RG), wt("vecs_g", 4, 5), ACT.Sqrt, bias=vec(V_BNEPS)).then_inc(roots_ready, 1)
            take_xs(0, 0)
            act.wait_ge(zeroed, 2)
            take_qk(0, 0)
            take_v(0, 0)
            take_xs(1, 1)
            exps(0, 0)
            attend(0, 0, before=False, second=False)
            attend(1, 1, second=False)
            with act.Fori(1, 3) as i:
                attend(2 * i, 0)
                attend(2 * i + 1, 1)
            attend(6, 0, coming=False)
            attend(7, 1, coming=False, after=False)
            a(small[0:BC, ROOT:ROOT + 1], vec(V_BNEPS), ACT.Sqrt)
            take_out(7)
            for m in (6, 7):
                square(1, m, m % 2, cen2_ready, sqr2_ready)
                act.wait_ge(var2_ready, m + 1)
                act.wait_ge(norm2_ready, m)
                a(rstd[:, 1, :], var[:, 1, :], ACT.Sqrt).then_inc(root2_ready, 1)

            for m in (6, 7):
                act.wait_ge(y_stored[m % 2], y_count(m))
            load_copies(act, 0, 1, PLANES5, C, (2,))

            def normed(n):
                act.wait_ge(w1_made, n + 1)
                for x, done in zip(stacked, (h_ready, h_doubled)):
                    a(chunk(x, n), bank(6 + n % 2)[0:BC], ACT.Identity, bias=col(T1), scale=col(S1)).then_inc(done, 1)

            act.wait_ge(folded, 1)
            for u in range(B * NCH):
                act.wait_ge(conv_made, u + 1)
                wait(act, gated_ready, u - 3)
                a(gel[:, u % 4, :], conv_bank(u)[0:64], ACT.Gelu).then_inc(gelu_ready, 1)
                c = u - (B - 1) * NCH
                if c >= 2:
                    normed(c - 2)
            normed(NCH - 2)
            normed(NCH - 1)

            def gelu_g(c, par):
                wait(act, w2_made, c - 1)
                for p in range(2):
                    act.wait_ge(wg_made, 2 * c + p + 1)
                    a(gg[:, par, p, :], bank(p)[0:BC], ACT.Gelu, bias=col(TG), scale=col(SG)).then_inc(gg_ready, 1)

            def gelu_f(c, par):
                wait(act, wf2_made, c - 1)
                for f in range(3):
                    act.wait_ge(wf1_made, 3 * c + f + 1)
                    a(gf[:, par, f, :], bank(3 + f), ACT.Gelu, bias=small[:, BF + f:BF + f + 1]).then_inc(gf_full, 1)
                for f in range(3):
                    act.wait_ge(gf_full, 3 * c + f + 1)
                    a(gfr[:, par, f, 0, :], gf[:, par, f, :], ACT.Copy).then_inc(gf_high, 1)

            gelu_g(0, 0)
            act.wait_ge(shift_ready, 1)
            def gelus(i):
                for u in range(2):
                    gelu_g(2 * i + u + 1, 1 - u)
                    gelu_f(2 * i + u, u)

            gelus(0)
            with act.Fori(1, 3) as i:
                gelus(i)
            gelu_g(7, 1)
            gelu_f(6, 0)
            gelu_f(7, 1)

        @block.vector
        def _(dve):
            v = nc.vector

            def centre(k, m, par):
                if k == 0:
                    src = (xtok[:, m, :] if isinstance(m, int) else xtok[:, bass.ds(m, 1), :].rearrange(
                        "p a n -> p (a n)")).rearrange("p (g c) -> p g c", c=C)
                    wait(dve, xhat_ready, m - 1)
                    wait(dve, cen_ready, m)
                    summed, done, dst = sum_ready, cen_ready, cen[:, par]
                else:
                    src = bank(7)[:, 0:TOK * BC].rearrange("p (g c) -> p g c", c=C)
                    dve.wait_ge(x1_turned, m + 1)
                    if isinstance(m, int) and m >= 5:
                        dve.wait_ge(y_ready, m - 1)
                    if isinstance(m, int) and m == NCH - 1:
                        dve.wait_ge(cen2_ready, m)
                    summed, done, dst = sum2_ready, cen2_ready, cen2[:, par]
                v.tensor_reduce(sums[:, k, :], src, AX.X, ALU.add).then_inc(summed, 1)
                dve.wait_ge(summed, m + 1)
                v.scalar_tensor_tensor(dst, sums[:, k, :].unsqueeze(2).to_broadcast([128, GR, C]), -1.0 / C, src,
                                       ALU.mult, ALU.add).then_inc(done, 1)

            def variance(k, m):
                squared_, summed, done = ((sqr_ready, ssq_ready, var_ready), (sqr2_ready, ssq2_ready, var2_ready))[k]
                dve.wait_ge(squared_, m + 1)
                v.tensor_reduce(squares[:, k, :], sqr[:, k], AX.X, ALU.add).then_inc(summed, 1)
                dve.wait_ge(summed, m + 1)
                v.tensor_scalar(var[:, k, :], squares[:, k, :], 1.0 / C, LN_EPS, ALU.mult, ALU.add).then_inc(done, 1)

            def normalise(k, m, par):
                deviation = rstd[:, k, :].unsqueeze(2).to_broadcast([128, GR, C])
                if k == 0:
                    if isinstance(m, int) and m < 2:
                        dve.wait_ge(root_ready, m + 1)
                        v.reciprocal(rstd[:, 0, :], rstd[:, 0, :]).then_inc(rstd_ready, 1)
                    dve.wait_ge(rstd_ready, m + 1)
                    wait(dve, xs_turned, m)
                    v.tensor_tensor(xhat[:, :, :].rearrange("p k (b c) -> p (k b) c", c=C), cen[:, par],
                                    deviation, ALU.mult).then_inc(xhat_ready, 1)
                else:
                    if isinstance(m, int) and m >= 6:
                        dve.wait_ge(root2_ready, m - 5)
                        v.reciprocal(rstd[:, 1, :], rstd[:, 1, :]).then_inc(rstd2_ready, 1)
                    dve.wait_ge(rstd2_ready, m + 1)
                    dve.wait_ge(gained_ready, m + 1)
                    v.tensor_tensor(cen2[:, par], gain_of(m), deviation, ALU.mult).then_inc(norm2_ready, 1)

            def subtract_max(m, w0):
                def by_head(w):
                    return bank(w % 2, 2 * NH * WT).rearrange("p (g k) -> p g k", k=WT)

                for w in (w0, w0 + 1):
                    dve.wait_ge(scores_made, WS * m + w + 1)
                    v.tensor_reduce(mx[:, w % 2, :], by_head(w), AX.X, ALU.max).then_inc(max_ready, 1)
                wait(dve, turned, 4 * m + w0 // 2 - 1)
                for w in (w0, w0 + 1):
                    dve.wait_ge(max_ready, WS * m + w + 1)
                    dst = diff[:, (w0 // 2) % 2, :, NH * WT * (w % 2):NH * WT * (w % 2 + 1)]
                    v.tensor_tensor(dst.rearrange("p i (h k) -> p i h k", k=WT),
                                    by_head(w).rearrange("p (i h) k -> p i h k", i=2),
                                    mx[:, w % 2, :].rearrange("p (i h) -> p i h", i=2).unsqueeze(3)
                                    .to_broadcast([128, 2, NH, WT]), ALU.subtract).then_inc(diff_ready, 1)

            def divide(m, half, par):
                g = 2 * m + half
                dve.wait_ge(mixed, 2 * g + 2)
                o = bank(4 + half, 12 * VW).rearrange("p (n c) -> p n c", c=VW)
                v.reciprocal(rz[:, half], o[:, :, 4 * HD:4 * HD + 2]).then_inc(rz_ready, 1)
                dve.wait_ge(rz_ready, g + 1)
                wait(dve, out_turned, m - 1)
                for j in range(2):
                    rows = slice(64 * j, 64 * j + 64)
                    l = v.tensor_tensor(ot[rows, par, half].rearrange("p n (x d) -> p n x d", d=HD),
                                        o[rows, :, 2 * HD * j:2 * HD * j + 2 * HD]
                                        .rearrange("p n (x d) -> p n x d", d=HD),
                                        rz[rows, half].unsqueeze(3).to_broadcast([64, 12, 2, HD]), ALU.mult)
                l.then_inc(ot_ready, 1)

            def residual(m, par):
                dve.wait_ge(projected, m + 1)
                if isinstance(m, int) and m >= 5:
                    dve.wait_ge(x1_ready, m - 1)
                src = bank(6)[0:BC].rearrange("p (w r s) -> p w r s", r=WS, s=WS)
                add = chunk(xin[0:BC], m).rearrange("p (w r s) -> p w r s", r=WS, s=WS)
                dst = x1s[:, par]
                cut = WS - SHIFT
                v.tensor_tensor(dst[:, :, SHIFT:W - cut].rearrange("p r (w s) -> p w r s", s=WS),
                                src[:, 0:WS - 1], add[:, 0:WS - 1], ALU.add)
                v.tensor_tensor(dst[:, :, W - cut:W], src[:, WS - 1, :, 0:cut], add[:, WS - 1, :, 0:cut], ALU.add)
                v.tensor_tensor(dst[:, :, 0:SHIFT], src[:, WS - 1, :, cut:], add[:, WS - 1, :, cut:], ALU.add)\
                    .then_inc(x1s_ready, 1)

            def copy_rows(m, par):
                wait(dve, v1_made, m - 1)
                v.tensor_copy(xs[BC:KX, par, :], chunk(xin[BC:KX], m)).then_inc(rows_ready, 1)

            def attend(m, par, coming=True, after=True, before=True, second=True):
                def ahead(l):
                    if after or l < 2:
                        subtract_max(m if l < 2 else m + 1, (2 * l + 4) % WS)

                ahead(0)
                if not after:
                    normalise(1, m - 3, 1 - par)
                if before:
                    divide(m - 1, 1, 1 - par)
                if coming:
                    centre(0, m + 2, par)
                ahead(1)
                if coming:
                    variance(0, m + 2)
                    copy_rows(m + 2, par)
                ahead(2)
                divide(m, 0, par)
                if coming:
                    normalise(0, m + 2, par)
                if second:
                    centre(1, m - 2, par)
                ahead(3)
                if second:
                    variance(1, m - 2)
                if before:
                    residual(m - 1, 1 - par)
                if not after:
                    divide(m, 1, par)
                if second and not (isinstance(m, int) and after):
                    normalise(1, m - 2, par)

            dve.wait_ge(first_x_in, 16)
            centre(0, 0, 0)
            centre(0, 1, 1)
            variance(0, 0)
            normalise(0, 0, 0)
            dve.wait_ge(rows_in, 16)
            copy_rows(0, 0)
            copy_rows(1, 1)
            variance(0, 1)
            dve.wait_ge(first_in, 16)
            dve.wait_ge(bias_in, 16)
            v.tensor_copy(posr[:, :], wt("posi"))
            places = [(odd, p, WT * i, WT * (NH - 1 - i if odd else i))
                      for odd in range(2) for i in range(NH) for p in range(2)]
            for odd, p, src, at in places:
                l = v.tensor_copy(biasr[0:WT, odd, p, at:at + WT], wt("rpb", src, src + WT))
            l.then_inc(bias_high, 1)
            dve.wait_ge(bias_high, 1)
            for odd, p, src, at in places:
                l = v.tensor_tensor(biasr[64:128, odd, p, at:at + WT], wt("rpb", src, src + WT),
                                    biasr[0:WT, odd, p, at:at + WT].bitcast(F32), ALU.subtract)
            l.then_inc(bias_ready, 1)
            dve.wait_ge(k_made, 1)
            for i in range(NH):
                dst, src = keys_of(i, 0)
                l = v.tensor_scalar(dst, src, wt("scales", i, i + 1), None, ALU.mult)
            l.then_inc(kmv_ready, 1)
            normalise(0, 1, 1)
            subtract_max(0, 0)
            subtract_max(0, 2)
            dve.wait_ge(x_in, 16)
            attend(0, 0, before=False, second=False)
            dve.wait_ge(weights_in, 16)
            dve.wait_ge(channels_in, 16)
            dve.wait_ge(roots_ready, 1)
            v.reciprocal(small[0:BC, R1:RG + 1], small[0:BC, R1:RG + 1]).then_inc(folding, 1)
            dve.wait_ge(folding, 1)
            norms = ((S1, R1, vec(V_G1), vec(V_B1), vec(V_M1), vec(V_BE1), T1),
                     (S2, R2, vec(V_G2), vec(V_B2), vec(V_M2), vec(V_BE2), T2),
                     (SG, RG, wt("vecs_g", 1, 2), wt("vecs_g", 0, 1), wt("vecs_g", 3, 4), wt("vecs_g", 2, 3), TG))
            for s, r, gain, b0, mean, beta, t in norms:
                v.tensor_tensor(col(s), col(r), gain, ALU.mult)
                l = v.tensor_tensor(col(t), b0, mean, ALU.subtract)
            l.then_inc(folding, 1)
            dve.wait_ge(folding, 2)
            for s, r, gain, b0, mean, beta, t in norms:
                l = v.scalar_tensor_tensor(col(t), col(t), col(s), beta, ALU.mult, ALU.add)
            v.tensor_tensor(wca[:, :], wt("pina"), wt("dwa"), ALU.mult)
            v.tensor_tensor(wcb[:, :], wt("pinb"), wt("dwb"), ALU.mult).then_inc(folded, 1)
            attend(1, 1, second=False)
            with dve.Fori(1, 3) as i:
                attend(2 * i, 0)
                attend(2 * i + 1, 1)
            attend(6, 0, coming=False)
            attend(7, 1, coming=False, after=False)
            centre(1, 6, 0)
            variance(1, 6)
            residual(7, 1)
            normalise(1, 6, 0)
            centre(1, 7, 1)
            dve.wait_ge(cen2_ready, NCH)
            dve.wait_ge(xs_turned, NCH)
            v.tensor_tensor(gain_of(7), cen2[:, 1], wt("gain2").unsqueeze(1).to_broadcast([128, GR, C]), ALU.mult)\
                .then_inc(gained_ready, 1)
            variance(1, 7)
            normalise(1, 7, 1)
            dve.wait_ge(norm2_ready, NCH)
            dve.wait_ge(y_stored[1], y_count(5))
            v.tensor_tensor(*shift_of(1), ALU.add).then_inc(last_y, 1)

            def edges(b, n):
                stack, rows = ((sta, RA), (stb, RB))[n]
                image = stack[:, b % 2].rearrange("k (h w) -> k h w", w=W)
                dve.wait_ge(stack_in[n][b % 2], stack_count(b, n))

                def mask(part, side):
                    return v.tensor_scalar(part, part, wt("edge", 4 * n + side, 4 * n + side + 1)[0:rows], None, ALU.mult)

                mask(image[:, 0, :], 2)
                mask(image[:, H - 1, :], 3).then_inc(bordered[n], 1)
                dve.wait_ge(bordered[n], b + 1)
                mask(image[:, :, 0:1], 0)
                mask(image[:, :, W - 1:W], 1).then_inc(edged[n], 1)

            edges(0, 0)
            for m in (6, 7):
                dve.wait_ge(y_stored[m % 2], y_count(m))
            dve.wait_ge(x1_ready, NCH)
            split = ((wf1r, "wf1"), (wf2r, "wf2"))
            for parts, name in split:
                l = v.tensor_copy(parts[:, 0, :], wt(name))
            l.then_inc(weights_high, 1)
            dve.wait_ge(weights_high, 1)
            for parts, name in split:
                v.tensor_tensor(parts[:, 1, :], wt(name), parts[:, 0, :].bitcast(F32), ALU.subtract)

            def row_minima(n):
                v.tensor_reduce(wmin[:, 8 * n:8 * n + 8, :],
                                chunk(stacked[0], n).rearrange("p (r x q) -> p r q x", q=2, x=W // 2), AX.X, ALU.min)

            def parity_minima(n):
                dve.wait_ge(h_ready, n + 1)
                here = chunk(stacked[0], n)
                part = hmin if n == 0 else hpart[:, n % 2]
                v.tensor_reduce(part[:, :, :], here.rearrange("p (r q w) -> p q w r", q=2, w=W), AX.X, ALU.min)\
                    .then_inc(hpart_ready, 1)
                if n < NCH - 3:
                    row_minima(n)
                if n:
                    dve.wait_ge(hpart_ready, n + 1)
                    v.tensor_tensor(hmin[:, :, :], hmin[:, :, :], hpart[:, n % 2], ALU.min).then_inc(hmin_ready, 1)
                    dve.wait_ge(hmin_ready, n)

            def nearest(i, par):
                c = 2 * i + par
                if isinstance(c, int) and c == 2:
                    dve.wait_ge(wg_made, 2)
                else:
                    wait(dve, xj_in[par], 32 * (i - 1 + par))
                wait(dve, xj_ready, c - 1)
                for q in range(2):
                    wm = wmin[:, bass.ts(c, 8), :].rearrange("p (r q) x -> p q r x", q=2)[:, q]
                    v.tensor_tensor(near[:, par].rearrange("p (r q) (w x) -> p q r w x", q=2, x=2)[:, q],
                                    hmin[:, q, :].rearrange("p (w x) -> p w x", x=2).unsqueeze(1)
                                    .to_broadcast([BC, 4, W // 2, 2]),
                                    wm.unsqueeze(2).to_broadcast([BC, 4, W // 2, 2]), ALU.min)\
                        .then_inc(near_ready, 1)
                dve.wait_ge(near_ready, 2 * (c + 1))
                v.tensor_tensor(xj[:, par, :], chunk(stacked[0], c), near[:, par].rearrange("p r w -> p (r w)"),
                                ALU.subtract).then_inc(xj_ready, 1)

            def second_residual(n):
                dve.wait_ge(pout_made, n + 1)
                v.tensor_tensor(chunk(x2, n), bank(4 + n % 2)[0:BC],
                                x1[:, 8 * n:8 * n + 8, :].rearrange("p r w -> p (r w)"), ALU.add)\
                    .then_inc(x2_ready, 1)

            edges(0, 1)
            for b in range(B):
                for c in range(NCH):
                    u = NCH * b + c
                    if c == NCH // 2 and b + 1 < B:
                        edges(b + 1, 0)
                        edges(b + 1, 1)
                    dve.wait_ge(gelu_ready, u + 1)
                    v.tensor_tensor(gated[64 * (b % 2):64 * (b % 2) + 64, b // 2, c * CH:(c + 1) * CH],
                                    conv_bank(u)[64:128], gel[:, u % 4, :], ALU.mult).then_inc(gated_ready, 1)
                    if b == B - 1 and c >= 1:
                        second_residual(c - 1)
                    if b == B - 1 and c >= 3:
                        parity_minima(c - 3)
            second_residual(NCH - 1)
            parity_minima(NCH - 3)
            parity_minima(NCH - 2)
            parity_minima(NCH - 1)
            nearest(0, 0)
            nearest(0, 1)
            for n in range(NCH - 3, NCH):
                row_minima(n)
            dve.wait_ge(shift_made, 1)
            v.tensor_tensor(small[:, BF:BF + 3], bank(3)[:, 0:3], wt("bf1"), ALU.add).then_inc(shift_ready, 1)

            def add_shortcut(c, par):
                dve.wait_ge(w2_made, c + 1)
                v.scalar_tensor_tensor(x3[:, par, :], bank(2)[0:BC], col(S2), chunk(x2, c), ALU.mult, ALU.add)\
                    .then_inc(x3_sum, 1)
                dve.wait_ge(x3_sum, c + 1)
                wait(dve, wf1_made, 3 * (c - 1))
                v.tensor_copy(x3r[:, par, 0, :], x3[:, par, :]).then_inc(x3_high, 1)
                dve.wait_ge(x3_high, c + 1)
                v.tensor_tensor(x3r[:, par, 1, :], x3[:, par, :], x3r[:, par, 0, :].bitcast(F32), ALU.subtract)\
                    .then_inc(x3_ready, 1)

            def finish(i, par):
                dve.wait_ge(wf2_made, 2 * i + par + 1)
                dve.wait_ge(stored[par], 16 * (i + 1))
                v.tensor_scalar(yo[:, par, :], bank(6)[0:BC], vec(V_BF2), None, ALU.add).then_inc(yo_ready, 1)

            def low_f(c, par):
                for f in range(2):
                    dve.wait_ge(gf_high, 3 * c + f + 1)
                    v.tensor_tensor(gfr[:, par, f, 1, :], gf[:, par, f, :], gfr[:, par, f, 0, :].bitcast(F32),
                                    ALU.subtract).then_inc(gf_low[0], 1)

            def chunk_step(i, par, early=True, late=True, before=True):
                c = 2 * i + par
                add_shortcut(c, par)
                if late:
                    nearest(i + 1, par)
                if early:
                    low_f(c - 1, 1 - par)
                if before:
                    finish(i - 1, par)

            chunk_step(0, 0, early=False, before=False)
            chunk_step(0, 1, before=False)
            with dve.Fori(1, 3) as i:
                chunk_step(i, 0)
                chunk_step(i, 1)
            chunk_step(3, 0, late=False)
            chunk_step(3, 1, late=False)
            low_f(7, 1)
            finish(3, 0)
            finish(3, 1)
    return nc


def lay_out(a):
    import numpy as np

    f = np.float32
    img, half = np.arange(B), np.arange(2)

    def blocks(w, rows=None, cols=None):
        o, n = w.shape
        m = np.zeros((B * n, B * o), f)
        for b in range(B):
            m[n * b:n * b + n, o * b:o * b + o] = w.T
        return m

    def stack_rows(n):
        count = STACKS[n][1] - STACKS[n][0]
        return [(slice(3 * count * y + z, 3 * count * (y + 1), 3), y, z) for y in range(3) for z in range(3)]

    x = np.roll(a["x"], (WS - SHIFT, -SHIFT), axis=(2, 3))
    x = x.reshape(BC, H // WS, WS, W // WS, WS).transpose(0, 1, 3, 2, 4).reshape(BC, NT)

    last_row = np.arange(H) >= H - SHIFT
    last_col = np.arange(W) >= W - SHIFT
    region = (2 * np.roll(last_row, WS)[:, None] + last_col[None, :]).reshape(H // WS, WS, W // WS, WS)
    region = region.transpose(0, 2, 1, 3).reshape(NT)
    feat = np.zeros((1 + NREG, NT), f)
    feat[0] = 1.0
    for r in range(NREG):
        feat[1 + r] = region == r

    qkv_w, qkv_b = a["L0_conv_qkv_w"], a["L0_conv_qkv_b"]
    p = {n: np.zeros(shape, f) for n, shape in PACK.items()}
    for b in range(B):
        rows = slice(C * b, C * b + C)
        p["wq"][rows, 32 * b:32 * b + C] = qkv_w[0:C].T
        p["wk"][rows, 32 * b:32 * b + C] = qkv_w[C:2 * C].T
        p["wv"][rows, rows] = qkv_w[2 * C:].T
        p["wq"][BC, 32 * b:32 * b + C] = qkv_b[0:C]
        p["wk"][BC, 32 * b:32 * b + C] = qkv_b[C:2 * C]
        p["wv"][BC, rows] = qkv_b[2 * C:]
        for r in range(NREG):
            p["wq"][BC + 1 + r, 32 * b + C + r] = 1.0
            p["wk"][BC, 32 * b + C + r] = MASKED
            p["wk"][BC + 1 + r, 32 * b + C + r] = -MASKED
            p["scales"][32 * b + C + r, :] = 1.0
        for i in range(NH):
            p["scales"][32 * b + HD * i:32 * b + HD * i + HD, i] = 1.0
        p["scales"][32 * b:32 * b + C, 3] = HD ** -0.5
        pair, j = divmod(b, 2)
        for y, (odd, i) in enumerate(place for halves in PLACES for place in halves):
            at, to = 2 * C * pair + HD * y, BC * (2 * odd + j) + C * b
            p["wproj"][at:at + HD, to:to + C] = a["L0_conv_proj_w"][:, HD * i:HD * i + HD].T
        for odd in range(2):
            p["wproj"][BC, 2 * BC * odd + C * b:2 * BC * odd + C * b + C] = a["L0_conv_proj_b"]
        p["pout"][64 * j:64 * j + HID, BC * pair + C * b:BC * pair + C * b + C] = a["L0_conv_pout_w"].T
        cols = slice(BC * pair + G2 * j, BC * pair + G2 * j + G2)
        p["wgh"][rows, cols] = a["L1_conv_wg"][:, 0:C].T
        p["wgx"][rows, cols] = a["L1_conv_wg"][:, C:].T
        other = slice(G2 * (1 - pair) + C * j, G2 * (1 - pair) + C * j + C)
        p["wg"][rows, cols] = a["L1_conv_wg"][:, 0:C].T
        p["wg"][other, cols] = a["L1_conv_wg"][:, C:].T
        p["w2"][G2 * j:G2 * j + G2, BC * pair + C * b:BC * pair + C * b + C] = a["L1_conv_w2"].T
        p["wf1"][rows, F4 * b:F4 * b + F4] = a["L1_conv_wf1"].T
    y, z = np.divmod(np.arange(WT), WS)
    at = (y[:, None] - y[None, :] + WS - 1) * (2 * WS - 1) + z[:, None] - z[None, :] + WS - 1
    p["rpb"][:] = a["L0_conv_rpb_table"][at].transpose(0, 2, 1).reshape(WT, NH * WT)
    p["posi"][:] = np.tile(np.eye(WT, dtype=f), (2, 2))
    p["eye"][:] = np.eye(128, dtype=f)
    per_channel = ["L0_conv_norm1_g", "L0_conv_norm1_b", "L1_conv_b1",
                   "L1_conv_g1", "L1_conv_be1", "L1_conv_m1", "L1_conv_v1", "L1_conv_b2", "L1_conv_g2",
                   "L1_conv_be2", "L1_conv_m2", "L1_conv_v2", "L1_conv_bf2"]
    for n, name in enumerate(per_channel):
        p["vecs"][:, n] = np.tile(a[name], B)
    p["gain2"][:], p["shift2"][:] = a["L0_conv_norm2_g"], a["L0_conv_norm2_b"]
    p["vecs"][:, V_BNEPS] = BN_EPS
    for n, name in enumerate(["bg", "gg", "beg", "mg", "vg"]):
        p["vecs_g"][:, n] = np.tile(a["L1_conv_" + name], 2)
    p["bf1"][:] = np.tile(a["L1_conv_bf1"], B).reshape(3, 128).T
    pin, taps = a["L0_conv_pin_w"], a["L0_conv_dw_w"].reshape(2 * HID, 9)
    for part in range(2):
        outs, src = slice(64 * part, 64 * part + HID), slice(HID * part, HID * part + HID)
        for n, (weights, taps_of) in enumerate((("pina", "dwa"), ("pinb", "dwb"))):
            for rows, y, z in stack_rows(n):
                p[weights][rows, outs] = pin[src, slice(*STACKS[n])].T
                p[taps_of][rows, outs] = taps[None, src, 3 * y + z]
    p["w1"][:] = blocks(a["L1_conv_w1"])
    p["wf2"][:] = blocks(a["L1_conv_wf2"]).reshape(3, 128, BC).transpose(1, 0, 2).reshape(128, 3 * BC)
    for n in range(2):
        for rows, y, z in stack_rows(n):
            p["edge"][rows, 4 * n:4 * n + 4] = (z != 0, z != 2, y != 0, y != 2)
    pack = np.zeros((128, PACK_W), f)
    for n, (r, c) in PACK.items():
        pack[0:r, PACK_AT[n]:PACK_AT[n] + c] = p[n]
    tokens = x.reshape(BC, NT // 128, 128).transpose(2, 1, 0).reshape(128, -1)
    return {"xw": np.ascontiguousarray(x), "xt": np.ascontiguousarray(tokens), "feat": feat, "pack": pack}


def kernel(**inputs):
    import numpy as np
    import concourse.bacc as bacc
    from concourse.bass_utils import run_bass_kernel_spmd

    arrays = lay_out({name: np.asarray(value) for name, value in inputs.items()})
    nc = bacc.Bacc("TRN2", target_bir_lowering=False, num_devices=1)
    args = [nc.dram_tensor(n, v.shape, F32, kind="ExternalInput").ap() for n, v in arrays.items()]
    out = nc.dram_tensor("out", (B, C, H, W), F32, kind="ExternalOutput").ap()
    build(nc, *args, out)
    return run_bass_kernel_spmd(nc, [arrays], core_ids=[0]).results[0]["out"]
```
